# Optimizing a Trainium2 kernel written in Bass

```python
import numpy as np
import jax
import jax.numpy as jnp

def _softmax(x, axis=-1):
    return jax.nn.softmax(x, axis=axis)

def _gelu(x):
    return jax.nn.gelu(x, approximate=True)

def _silu(x):
    return jax.nn.silu(x)

def _sigmoid(x):
    return jax.nn.sigmoid(x)

def _layernorm(x, axis=-1, eps=1e-05):
    m = jnp.mean(x, axis=axis, keepdims=True)
    v = jnp.var(x, axis=axis, keepdims=True)
    return (x - m) / jnp.sqrt(v + eps)

def _scatter_add(tgt, idx, src, axis=0):
    return tgt.at[idx].add(src)

def _segment_sum(src, seg, n):
    return jax.ops.segment_sum(src, seg, n)
kernel_name = 'mk_lm_tower_d1_tok_ids1024_r4_bd65de'

def setup_inputs(seed: int=0):
    np.random.seed(seed)
    _w = jnp.asarray

    def _rec_inputs():
        import jax
        import jax.numpy as jnp
        _rk = jax.random.key(seed)
        x = jax.random.randint(jax.random.fold_in(_rk, 1), (32, 128), 0, 127987, jnp.int32)
        return x
    x = _rec_inputs()

    def _L0_tok_setup():
        import jax, jax.numpy as jnp
        import numpy as np
        N_TOKENS = 32000
        D_EMBED = 256
        D_PROJ = 256
        CUTOFF_ENDS = [0, 5000, 15000, 25000, N_TOKENS]
        DIV_VAL = 4
        EMB_SCALE = D_PROJ ** 0.5
        key = jax.random.key(seed)
        keys = jax.random.split(key, 9)
        inp = {'input': jax.random.randint(keys[0], (4, 512), 0, N_TOKENS, dtype=jnp.int64) if jax.config.jax_enable_x64 else jax.random.randint(keys[0], (4, 512), 0, N_TOKENS, dtype=jnp.int32)}
        for i in range(4):
            left, right = (CUTOFF_ENDS[i], CUTOFF_ENDS[i + 1])
            d_emb_i = D_EMBED // DIV_VAL ** i
            inp[f'emb{i}'] = jax.random.normal(keys[1 + i], (right - left, d_emb_i), dtype=jnp.float32)
            inp[f'proj{i}'] = jax.random.normal(keys[5 + i], (D_PROJ, d_emb_i), dtype=jnp.float32)
        return inp
    _L0_tok_all = _L0_tok_setup()
    _L0_tok_in = {k: v for k, v in _L0_tok_all.items() if k in ('emb0', 'emb1', 'emb2', 'emb3', 'proj0', 'proj1', 'proj2', 'proj3')}
    del _L0_tok_all

    def _L0_attn_setup():
        import jax, jax.numpy as jnp
        import numpy as np
        from jax import lax
        D_MODEL = 256
        D_STATE = 16
        BATCH = 8
        SEQ = 512

        def _silu(x):
            return x * jax.nn.sigmoid(x)

        def _depthwise_conv(x, conv_w):
            xc = jnp.swapaxes(x, 1, 2)
            y = lax.conv_general_dilated(xc, conv_w, window_strides=(1,), padding=[(1, 1)], dimension_numbers=('NCH', 'OIH', 'NCH'), feature_group_count=conv_w.shape[0])
            return jnp.swapaxes(y, 1, 2)

        def _ssm(x, A, B_ssm, C_ssm, D_ssm):
            Abar = jax.nn.sigmoid(A)
            b, l, c = x.shape
            h0 = jnp.zeros((b, c, A.shape[1]), x.dtype)

            def step(h, xt):
                h = h * Abar + xt[..., None] * B_ssm
                y = jnp.einsum('bcs,cs->bc', h, C_ssm) + D_ssm * xt
                return (h, y)
            _, ys = lax.scan(step, h0, jnp.swapaxes(x, 0, 1))
            return jnp.swapaxes(ys, 0, 1)
        key = jax.random.key(seed)
        ks = jax.random.split(key, 12)
        s = 0.02
        return {'x': jax.random.normal(ks[0], (BATCH, SEQ, D_MODEL), jnp.float32), 'w1_w': jax.random.normal(ks[1], (D_MODEL, D_MODEL), jnp.float32) * s, 'w1_b': jnp.zeros((D_MODEL,), jnp.float32), 'v1_w': jax.random.normal(ks[2], (D_MODEL, D_MODEL), jnp.float32) * s, 'v1_b': jnp.zeros((D_MODEL,), jnp.float32), 'w2_w': jax.random.normal(ks[3], (D_MODEL, D_MODEL), jnp.float32) * s, 'w2_b': jnp.zeros((D_MODEL,), jnp.float32), 'conv_w': jax.random.normal(ks[4], (D_MODEL, 1, 3), jnp.float32) * s, 'A': jax.random.normal(ks[5], (D_MODEL, D_STATE), jnp.float32), 'B_ssm': jax.random.normal(ks[6], (D_MODEL, D_STATE), jnp.float32) * s, 'C_ssm': jax.random.normal(ks[7], (D_MODEL, D_STATE), jnp.float32) * s, 'D_ssm': jnp.ones((D_MODEL,), jnp.float32)}
    _L0_attn_all = _L0_attn_setup()
    _L0_attn_in = {k: v for k, v in _L0_attn_all.items() if k in ('w1_w', 'w1_b', 'v1_w', 'v1_b', 'w2_w', 'w2_b', 'conv_w', 'A', 'B_ssm', 'C_ssm', 'D_ssm')}
    del _L0_attn_all

    def _L0_ffn_setup():
        import jax, jax.numpy as jnp
        import numpy as np
        E = 8
        TOPK = 2
        PRIME = 11
        HASH_OFF = 7919
        N_SHARED = 1
        key = jax.random.key(seed)
        ks = jax.random.split(key, 8)
        B, T, C, Hs, Hr = (4, 2048, 256, 512, 256)
        sc = lambda k, shape, fan: jax.random.normal(k, shape, jnp.float32) * fan ** (-0.5)
        return {'x': jax.random.normal(ks[0], (B, T, C), jnp.float32), 't_emb': jax.random.normal(ks[1], (B, C), jnp.float32), 'sw1': sc(ks[2], (C, Hs), C), 'sb1': jnp.zeros((Hs,), jnp.float32), 'sw3': sc(ks[3], (C, Hs), C), 'sb3': jnp.zeros((Hs,), jnp.float32), 'sw2': sc(ks[4], (Hs, C), Hs), 'sb2': jnp.zeros((C,), jnp.float32), 'w1': sc(ks[5], (E, C, Hr), C), 'b1': jnp.zeros((E, Hr), jnp.float32), 'w2': sc(ks[6], (E, Hr, C), Hr), 'b2': jnp.zeros((E, C), jnp.float32)}
    _L0_ffn_all = _L0_ffn_setup()
    _L0_ffn_in = {k: v for k, v in _L0_ffn_all.items() if k in ('t_emb', 'sw1', 'sb1', 'sw3', 'sb3', 'sw2', 'sb2', 'w1', 'b1', 'w2', 'b2')}
    del _L0_ffn_all
    return {'x': x, 'L0_tok_emb0': _L0_tok_in['emb0'], 'L0_tok_emb1': _L0_tok_in['emb1'], 'L0_tok_emb2': _L0_tok_in['emb2'], 'L0_tok_emb3': _L0_tok_in['emb3'], 'L0_tok_proj0': _L0_tok_in['proj0'], 'L0_tok_proj1': _L0_tok_in['proj1'], 'L0_tok_proj2': _L0_tok_in['proj2'], 'L0_tok_proj3': _L0_tok_in['proj3'], 'L0_attn_w1_w': _L0_attn_in['w1_w'], 'L0_attn_w1_b': _L0_attn_in['w1_b'], 'L0_attn_v1_w': _L0_attn_in['v1_w'], 'L0_attn_v1_b': _L0_attn_in['v1_b'], 'L0_attn_w2_w': _L0_attn_in['w2_w'], 'L0_attn_w2_b': _L0_attn_in['w2_b'], 'L0_attn_conv_w': _L0_attn_in['conv_w'], 'L0_attn_A': _L0_attn_in['A'], 'L0_attn_B_ssm': _L0_attn_in['B_ssm'], 'L0_attn_C_ssm': _L0_attn_in['C_ssm'], 'L0_attn_D_ssm': _L0_attn_in['D_ssm'], 'L0_ffn_t_emb': _L0_ffn_in['t_emb'], 'L0_ffn_sw1': _L0_ffn_in['sw1'], 'L0_ffn_sb1': _L0_ffn_in['sb1'], 'L0_ffn_sw3': _L0_ffn_in['sw3'], 'L0_ffn_sb3': _L0_ffn_in['sb3'], 'L0_ffn_sw2': _L0_ffn_in['sw2'], 'L0_ffn_sb2': _L0_ffn_in['sb2'], 'L0_ffn_w1': _L0_ffn_in['w1'], 'L0_ffn_b1': _L0_ffn_in['b1'], 'L0_ffn_w2': _L0_ffn_in['w2'], 'L0_ffn_b2': _L0_ffn_in['b2']}

def reference(x, L0_tok_emb0, L0_tok_emb1, L0_tok_emb2, L0_tok_emb3, L0_tok_proj0, L0_tok_proj1, L0_tok_proj2, L0_tok_proj3, L0_attn_w1_w, L0_attn_w1_b, L0_attn_v1_w, L0_attn_v1_b, L0_attn_w2_w, L0_attn_w2_b, L0_attn_conv_w, L0_attn_A, L0_attn_B_ssm, L0_attn_C_ssm, L0_attn_D_ssm, L0_ffn_t_emb, L0_ffn_sw1, L0_ffn_sb1, L0_ffn_sw3, L0_ffn_sb3, L0_ffn_sw2, L0_ffn_sb2, L0_ffn_w1, L0_ffn_b1, L0_ffn_w2, L0_ffn_b2):
    import jax
    import jax.numpy as jnp

    def _L0_tok_ref(input, emb0, emb1, emb2, emb3, proj0, proj1, proj2, proj3):
        import jax, jax.numpy as jnp
        import numpy as np
        N_TOKENS = 32000
        D_EMBED = 256
        D_PROJ = 256
        CUTOFF_ENDS = [0, 5000, 15000, 25000, N_TOKENS]
        DIV_VAL = 4
        EMB_SCALE = D_PROJ ** 0.5
        tables = [emb0, emb1, emb2, emb3]
        projs = [proj0, proj1, proj2, proj3]
        flat = input.reshape(-1)
        out = jnp.zeros((flat.shape[0], D_PROJ), dtype=jnp.float32)
        for i in range(4):
            left, right = (CUTOFF_ENDS[i], CUTOFF_ENDS[i + 1])
            mask = (flat >= left) & (flat < right)
            idx = jnp.clip(flat - left, 0, right - left - 1)
            e = jnp.einsum('td,pd->tp', tables[i][idx], projs[i])
            out = out + jnp.where(mask[:, None], e, 0.0)
        out = out * jnp.asarray(EMB_SCALE, out.dtype)
        return out.reshape(*input.shape, D_PROJ)

    def _L0_attn_ref(x, w1_w, w1_b, v1_w, v1_b, w2_w, w2_b, conv_w, A, B_ssm, C_ssm, D_ssm):
        import jax, jax.numpy as jnp
        import numpy as np
        from jax import lax
        D_MODEL = 256
        D_STATE = 16
        BATCH = 8
        SEQ = 512

        def _silu(x):
            return x * jax.nn.sigmoid(x)

        def _depthwise_conv(x, conv_w):
            xc = jnp.swapaxes(x, 1, 2)
            y = lax.conv_general_dilated(xc, conv_w, window_strides=(1,), padding=[(1, 1)], dimension_numbers=('NCH', 'OIH', 'NCH'), feature_group_count=conv_w.shape[0])
            return jnp.swapaxes(y, 1, 2)

        def _ssm(x, A, B_ssm, C_ssm, D_ssm):
            Abar = jax.nn.sigmoid(A)
            b, l, c = x.shape
            h0 = jnp.zeros((b, c, A.shape[1]), x.dtype)

            def step(h, xt):
                h = h * Abar + xt[..., None] * B_ssm
                y = jnp.einsum('bcs,cs->bc', h, C_ssm) + D_ssm * xt
                return (h, y)
            _, ys = lax.scan(step, h0, jnp.swapaxes(x, 0, 1))
            return jnp.swapaxes(ys, 0, 1)
        x1 = x @ w1_w.T + w1_b
        x_conv = _silu(_depthwise_conv(x1, conv_w))
        x_ssm = _ssm(x_conv, A, B_ssm, C_ssm, D_ssm)
        v = _silu(x @ v1_w.T + v1_b)
        return x_ssm * v @ w2_w.T + w2_b

    def _L0_ffn_ref(x, t_emb, sw1, sb1, sw3, sb3, sw2, sb2, w1, b1, w2, b2):
        import jax, jax.numpy as jnp
        import numpy as np
        E = 8
        TOPK = 2
        PRIME = 11
        HASH_OFF = 7919
        N_SHARED = 1
        B, T, C = x.shape
        N = B * T
        xf = x.reshape(N, C)
        shared = jax.nn.silu(xf @ sw1 + sb1) * (xf @ sw3 + sb3) @ sw2 + sb2
        tok = jnp.arange(N)
        out = jnp.zeros((N, C), x.dtype)
        for k in range(TOPK):
            exp_ids = (tok * PRIME + k * HASH_OFF) % E
            sort_idx = jnp.argsort(exp_ids)
            xs = xf[sort_idx].reshape(E, N // E, C)
            h = jax.nn.gelu(jnp.einsum('enc,ech->enh', xs, w1) + b1[:, None, :], approximate=False)
            y = jnp.einsum('enh,ehc->enc', h, w2) + b2[:, None, :]
            out = out.at[sort_idx].add(y.reshape(N, C))
        out = out / TOPK
        return ((shared + out) / (N_SHARED + 1)).reshape(B, T, C)
    h = _L0_tok_ref(x, L0_tok_emb0, L0_tok_emb1, L0_tok_emb2, L0_tok_emb3, L0_tok_proj0, L0_tok_proj1, L0_tok_proj2, L0_tok_proj3)
    h = h + _L0_attn_ref(_layernorm(h, axis=-1), L0_attn_w1_w, L0_attn_w1_b, L0_attn_v1_w, L0_attn_v1_b, L0_attn_w2_w, L0_attn_w2_b, L0_attn_conv_w, L0_attn_A, L0_attn_B_ssm, L0_attn_C_ssm, L0_attn_D_ssm)
    h = h + _L0_ffn_ref(_layernorm(h, axis=-1), L0_ffn_t_emb, L0_ffn_sw1, L0_ffn_sb1, L0_ffn_sw3, L0_ffn_sb3, L0_ffn_sw2, L0_ffn_sb2, L0_ffn_w1, L0_ffn_b1, L0_ffn_w2, L0_ffn_b2)
    return h

_drawn_inputs = setup_inputs


def setup_inputs(seed=0):
    import zlib

    import numpy as np

    out = dict(_drawn_inputs(seed))
    spreads = {'L0_attn_w1_b': (0.0, 0.8),
     'L0_attn_v1_b': (0.0, 0.8),
     'L0_attn_w2_b': (0.0, 0.8),
     'L0_attn_D_ssm': (1.0, 0.6),
     'L0_ffn_sb1': (0.0, 0.8),
     'L0_ffn_sb3': (0.0, 0.8),
     'L0_ffn_sb2': (0.0, 0.8),
     'L0_ffn_b1': (0.0, 0.8),
     'L0_ffn_b2': (0.0, 0.8)}
    factors = {'L0_attn_w1_w': 8.0,
     'L0_attn_v1_w': 8.0,
     'L0_attn_w2_w': 8.0,
     'L0_attn_conv_w': 8.0,
     'L0_attn_A': 8.0,
     'L0_attn_B_ssm': 8.0,
     'L0_attn_C_ssm': 8.0,
     'L0_ffn_sw1': 8.0,
     'L0_ffn_sw3': 8.0,
     'L0_ffn_sw2': 8.0,
     'L0_ffn_w1': 8.0,
     'L0_ffn_w2': 8.0}
    for name, (base, spread) in spreads.items():
        noise = np.random.default_rng([zlib.crc32(name.encode()), seed]).standard_normal(out[name].shape)
        drawn = base * np.exp(spread * noise) if base else spread * noise
        out[name] = jnp.asarray(drawn.astype(out[name].dtype))
    for name, factor in factors.items():
        out[name] = (out[name] * factor).astype(out[name].dtype)
    return out
```

```python
from contextlib import ExitStack

import concourse.bass as bass
from concourse import mybir

F32 = mybir.dt.float32
F32R = mybir.dt.float32r
F16 = mybir.dt.float16
I32 = mybir.dt.int32
ALU = mybir.AluOpType
ACT = mybir.ActivationFunctionType
AX_X = mybir.AxisListType.X

P = 128
BATCH, SEQ, D = 32, 128, 256
VOCAB = 32000
CAT = 384
KC = CAT // P
HALVES = D // P
RES = 8
GROUPS = BATCH * SEQ // (P * RES)
GTOK = P * RES
BLK = 512
STATES = 16
HS = 512
HR = 256
UNITS = 8
EMB_SCALE = float(D) ** 0.5
EPS = 1e-5
CH = 16
NQ = D // CH
TRING = 3
YLEN = 256

C_W1B, C_V1B, C_CONV = 0, 2, 4
C_A, C_B, C_C, C_D = 10, 42, 74, 106
C_SB1, C_SB3, C_B1 = 108, 112, 116
NSMALL = 132

OLD, SHARED, NEW = range(3)
PLAN = [(OLD, 0, 0), (OLD, 1, 1), (SHARED, 0, 2), (SHARED, 1, 0), (SHARED, 2, 2), (SHARED, 3, 0), (NEW, 0, 2), (NEW, 1, 3)]


def slot_of(r):
    return 3 * r % RES


def tower(nc, ids, table, small, rows, w_a, w_b, w_e, kernel_rows, out):
    ctx = ExitStack()
    with ctx:
        _tower(nc, ctx, ids, table, small, rows, w_a, w_b, w_e, kernel_rows, out)


def _tower(nc, ctx, ids, table, small, rows, w_a, w_b, w_e, kernel_rows, out):
    def sem(name):
        return ctx.enter_context(nc.semaphore(name))

    def sb(stack, name, shape, dt, side):
        return stack.enter_context(nc.sbuf_tensor(name, shape, dt, side=side))

    R, L = "right", "left"
    h_sb = sb(ctx, "h_sb", [P, GROUPS, RES, D], F32, R)
    v_sb = sb(ctx, "v_sb", [P, HALVES, BATCH * SEQ], F32, R)
    w2_hi = sb(ctx, "w2_hi", [P, HALVES, D], F32R, R)
    w2_lo = sb(ctx, "w2_lo", [P, HALVES, D], F32R, R)
    bias_e = sb(ctx, "bias_e", [P, RES, D], F32, R)
    vec = sb(ctx, "vec", [P, NSMALL], F32, R)
    ident = sb(ctx, "ident", [P, P], F32, R)
    stat = sb(ctx, "stat", [P, 4, 6], F32, R)
    mv = sb(ctx, "mv", [P, 4, 2], F32, R)
    rstd = sb(ctx, "rstd", [P, 4], F32, R)
    minus_half = sb(ctx, "minus_half", [P, 1], F32, R)

    ssm_mem = ExitStack()
    x_hi = sb(ssm_mem, "x_hi", [P, D, BATCH], F16, R)
    x_lo = sb(ssm_mem, "x_lo", [P, D, BATCH], F16, R)
    toep = sb(ssm_mem, "toep", [P, TRING, CH, SEQ, 2], F16, R)
    flat = toep[:, :, :, :, :].rearrange("p a c t w -> p (a c t w)").bitcast(F32)
    power = flat[:, 0:HALVES * STATES * SEQ].rearrange("p (s t) -> p s t", t=SEQ)
    raw_at = HALVES * STATES * SEQ
    raw_a = flat[:, raw_at:raw_at + (KC + 4) * D]
    k_sum = flat[:, raw_at + (KC + 4) * D:raw_at + (KC + 5) * D].rearrange("p (h t) -> p h t", t=SEQ)

    mem_a = ExitStack()
    row_in = sb(mem_a, "row_in", [P, 3, D], F32, L)
    x_ids = sb(mem_a, "x_ids", [P, GROUPS, RES], I32, L)
    idx = sb(mem_a, "idx", [P, RES], I32, L)
    cat = sb(mem_a, "cat", [P, RES, CAT], F32, L)
    catT_hi = sb(mem_a, "catT_hi", [P, 2, KC, P], F32R, L)
    catT_lo = sb(mem_a, "catT_lo", [P, 2, KC, P], F32R, L)
    hn = sb(mem_a, "hn", [P, 4, D], F32, L)
    hnT_hi = sb(mem_a, "hnT_hi", [P, HALVES, GTOK], F32R, L)
    hnT_lo = sb(mem_a, "hnT_lo", [P, HALVES, GTOK], F32R, L)
    x_pad = sb(mem_a, "x_pad", [P, 2, 4, SEQ + 2], F32, L)
    x_mid = sb(mem_a, "x_mid", [P, 2, 4, SEQ], F32, L)
    x_sil = sb(mem_a, "x_sil", [P, 4, 4, SEQ], F32, L)
    proj_hi = sb(mem_a, "proj_hi", [P, KC, D], F32R, L)
    proj_lo = sb(mem_a, "proj_lo", [P, KC, D], F32R, L)
    wv_hi = sb(mem_a, "wv_hi", [P, 2, HALVES, D], F32R, L)
    wv_lo = sb(mem_a, "wv_lo", [P, 2, HALVES, D], F32R, L)
    abar = sb(mem_a, "abar", [P, 7, HALVES * STATES], F32, L)
    bc = sb(mem_a, "bc", [P, HALVES * STATES], F32, L)
    k_row = sb(mem_a, "k_row", [P, HALVES, YLEN, 2], F16, L)
    mem_a.close()

    mem_b = ctx
    sw_hi = sb(mem_b, "sw_hi", [P, 6, BLK], F32R, L)
    sw_lo = sb(mem_b, "sw_lo", [P, 6, BLK], F32R, L)
    ex0_hi = sb(mem_b, "ex0_hi", [P, 2, BLK], F32R, L)
    ex0_lo = sb(mem_b, "ex0_lo", [P, 2, BLK], F32R, L)
    stage = sb(mem_b, "stage", [P, 4, BLK], F32, L)
    mem_y = ExitStack()
    y_sb = sb(mem_y, "y_sb", [P, BATCH, D], F32, L)
    mem_y.close()
    ssm_mem.close()

    ex1_hi = sb(ctx, "ex1_hi", [P, 2, BLK], F32R, R)
    ex1_lo = sb(ctx, "ex1_lo", [P, 2, BLK], F32R, R)
    zc_hi = sb(ctx, "zc_hi", [P, 2, HALVES, P], F32R, R)
    zc_lo = sb(ctx, "zc_lo", [P, 2, HALVES, P], F32R, R)
    h2n = sb(ctx, "h2n", [P, 4, D], F32, R)
    h2nT_hi = sb(ctx, "h2nT_hi", [P, 2, HALVES, BLK], F32R, R)
    h2nT_lo = sb(ctx, "h2nT_lo", [P, 2, HALVES, BLK], F32R, R)
    hid_hi = sb(ctx, "hid_hi", [P, 4, BLK], F32R, R)
    hid_lo = sb(ctx, "hid_lo", [P, 4, BLK], F32R, R)
    act_out = sb(ctx, "act_out", [P, 4, BLK], F32, R)
    o_sb = sb(ctx, "o_sb", [P, 2, GROUPS, D], F32, R)
    ex_hi, ex_lo = [ex0_hi, ex1_hi], [ex0_lo, ex1_lo]

    ps = [ctx.enter_context(nc.psum_tensor(f"ps{i}", [P, BLK], F32)) for i in range(8)]

    ids_in = sem("ids_in")
    vec_in = sem("vec_in")
    wa_in = sem("wa_in")
    rows_in = sem("rows_in")
    ident_step = sem("ident_step")
    half_set = sem("half_set")
    pad_zero = sem("pad_zero")
    wa_hi = sem("wa_hi")
    wa_lo = sem("wa_lo")
    abar_done = sem("abar_done")
    k_step = sem("k_step")
    k_out = sem("k_out")
    bias_step = sem("bias_step")
    idx_copied = sem("idx_copied")
    cat_zero = sem("cat_zero")
    gathered = [sem(f"gathered{r}") for r in range(RES)]
    cat_tr = sem("cat_tr")
    catT_hi_done = sem("catT_hi_done")
    catT_lo_done = sem("catT_lo_done")
    emb_done = sem("emb_done")
    h_done = sem("h_done")
    stats_done = sem("stats_done")
    aggr_done = sem("aggr_done")
    eps_done = sem("eps_done")
    rstd_done = sem("rstd_done")
    hn_done = sem("hn_done")
    tp_filled = sem("tp_filled")
    tp_hi_done = sem("tp_hi_done")
    tp_lo_done = sem("tp_lo_done")
    mm_done = sem("mm_done")
    mm_evac = sem("mm_evac")
    mid_done = sem("mid_done")
    conv_left = sem("conv_left")
    conv_done = sem("conv_done")
    sil_done = sem("sil_done")
    toep_in = [sem(f"toep_in{s}") for s in range(TRING)]
    ssm_done = sem("ssm_done")
    y_act = sem("y_act")
    y_dve = sem("y_dve")
    yt_filled = sem("yt_filled")
    z_done = sem("z_done")
    stage_in = [sem(f"stage_in{s}") for s in range(4)]
    w_scaled = sem("w_scaled")
    w_hi_done = sem("w_hi_done")
    w_lo_done = sem("w_lo_done")
    h_biased = sem("h_biased")
    ex_in = [sem(f"ex_in{s}") for s in range(2)]
    ex_hi_done = sem("ex_hi_done")
    ex_done = sem("ex_done")
    zc_hi_done = sem("zc_hi_done")
    zc_lo_done = sem("zc_lo_done")
    w2_done = sem("w2_done")
    h2_done = sem("h2_done")
    stats2_done = sem("stats2_done")
    aggr2_done = sem("aggr2_done")
    eps2_done = sem("eps2_done")
    rstd2_done = sem("rstd2_done")
    h2n_done = sem("h2n_done")
    h2_biased = sem("h2_biased")
    tr2_done = sem("tr2_done")
    h2nT_hi_done = sem("h2nT_hi_done")
    h2nT_lo_done = sem("h2nT_lo_done")
    up_done = sem("up_done")
    act_done = sem("act_done")
    gated = sem("gated")
    hid_hi_done = sem("hid_hi_done")
    hid_lo_done = sem("hid_lo_done")
    l2_done = sem("l2_done")
    o_done = sem("o_done")
    stored = [sem(f"stored{s}") for s in range(2)]

    def f32(ap):
        return ap.bitcast(F32)

    def wait_alone(eng, signal, count, passed, value=1):
        if not isinstance(count, int):
            eng.compute_val(count)
            eng.wait_ge(passed, value)
        eng.wait_ge(signal, count)

    def tp_before(i):
        return 8 * i - 4 if not isinstance(i, int) or i > 0 else 0

    def turns(i):
        if isinstance(i, int) and i == 0:
            return [("hn", 0), ("hn", 1), ("hn", 2), ("hn", 3)]
        return [("hn", 0), ("hn", 1), ("x", 0), ("x", 1), ("hn", 2), ("x", 2), ("x", 3), ("hn", 3)]

    def turn_no(i, what):
        return tp_before(i) + turns(i).index(what)

    def body_order(i):
        first = isinstance(i, int) and i == 0
        x = (lambda *us: []) if first else (lambda *us: [("x", u) for u in us])
        steps = [("cat", 0)]
        for r in range(1, RES):
            steps += [("cat", r), ("emb", r - 1)]
            if r in (4, 6):
                steps.append(("hn", (r - 4) // 2))
        return steps + x(0, 1) + [("emb", RES - 1), ("hn", 2)] + x(2, 3) + [("hn", 3)]

    K_STEPS = 2 + 7 + 6 + 1 + 1 + 1 + 1 + 1 + 1

    def hn_bank(bank):
        return bank[:, :].rearrange("c (r h p) -> c h p r", r=2, h=HALVES)

    def hnT_at(t, pair):
        return t[:, :, :].rearrange("c h (p r) -> c h p r", r=RES)[:, :, :, 2 * pair:2 * pair + 2]

    def x_bank(bank):
        return bank[:, :].rearrange("u (b c) -> u b c", b=4)

    def x_at(t, i, u):
        k, half = u // 2, u % 2
        v = t[:, half * P:(half + 1) * P, :].rearrange("u c b -> u b c")
        return v[:, bass.ds(8 * i + 4 * k, 4), :]

    def y_bank(q):
        return ps[q % 4][:, :].rearrange("t (c b) -> t c b", c=CH)

    def y_at(q):
        return y_sb[:, :, q * CH:(q + 1) * CH].rearrange("t b c -> t c b")

    def tr2_bank():
        return ps[7][:, 0:D].rearrange("c (h p) -> c h p", h=HALVES)

    def z_cols(e, g):
        r = (3 * e) & (RES - 1)
        v = v_sb[:, :, g * GTOK:(g + 1) * GTOK].rearrange("c h (p r) -> c h r p", r=RES)
        return v[:, :, bass.ds(r, 1), :].rearrange("c h o p -> c h (o p)")

    TP = [ps[4], ps[5]]
    MM = [ps[6], ps[7]]
    block = ctx.enter_context(nc.Block())

    @block.sync
    def _(sp):
        sp.dma_start(x_ids[:, :, :], ids.rearrange("(g p r) -> p g r", p=P, r=RES)).then_inc(ids_in, 16)
        sp.dma_start(raw_a, w_a).then_inc(wa_in, 16)
        sp.dma_start(vec[:, :], small).then_inc(vec_in, 16)
        sp.dma_start(row_in[:, 0:2, :], bass.AP(rows.tensor, 0, [[0, P], [D, 2], [1, D]])).then_inc(rows_in, 16)
        sp.dma_start(bias_e[:, :, :], bass.AP(rows.tensor, 2 * D, [[0, P], [D, RES], [1, D]])).then_inc(rows_in, 16)
        sp.wait_ge(k_step, K_STEPS)
        sp.dma_start(kernel_rows.rearrange("(h p) n -> p h n", p=P),
                     k_row[:, :, :, :].rearrange("p h n w -> p h (n w)").bitcast(F32)).then_inc(k_out, 16)
        sp.wait_ge(k_out, 16)
        for q in range(NQ):
            if q < TRING:
                sp.wait_ge(wa_lo, 1)
            else:
                sp.wait_ge(ssm_done, q - TRING + 1)
            src = bass.AP(kernel_rows.tensor, q * CH * YLEN, [[1, P], [YLEN, CH], [1, SEQ]])
            dst = toep[:, q % TRING, :, :, :].rearrange("p c t w -> p c (t w)").bitcast(F32)
            sp.dma_start(dst, src).then_inc(toep_in[q % TRING], 16)

        def store(e, par):
            wait_alone(sp, o_done, GROUPS * e + GROUPS, ids_in, 16)
            r = (3 * e) & (RES - 1)
            dst = out.rearrange("(g p r) c -> r p g c", p=P, r=RES)
            sp.dma_start(dst[bass.ds(r, 1), :, :, :].rearrange("o p g c -> (o p) g c"),
                         o_sb[:, par, :, :]).then_inc(stored[par], 16)

        store(0, 0)
        with sp.Fori(0, (RES - 2) // 2) as i:
            store(2 * i + 1, 1)
            store(2 * i + 2, 0)
        store(RES - 1, 1)
        sp.wait_ge(stored[0], 16 * RES // 2)
        sp.wait_ge(stored[1], 16 * RES // 2)

    @block.gpsimd
    def _(pool):
        nc.gpsimd.memset(ident[:, :], 0.0).then_inc(ident_step, 1)
        nc.gpsimd.memset(minus_half[:, :], -0.5).then_inc(half_set, 1)
        pool.wait_ge(ident_step, 1)
        nc.gpsimd.affine_select(out=ident[:, :], in_=ident[:, :], compare_op=ALU.not_equal, fill=1.0, base=0,
                                pattern=[[-1, P]], channel_multiplier=1).then_inc(ident_step, 1)
        pool.wait_ge(ids_in, 16)

        def power_step(n, m, s_eps, s_rstd):
            wait_alone(pool, s_eps, n + 1, half_set)
            nc.gpsimd.tensor_tensor(rstd[:, m:m + 1], rstd[:, m:m + 1], minus_half[:, :], ALU.pow).then_inc(s_rstd, 1)

        def ids_of(i):
            if not (isinstance(i, int) and i == 0):
                for r in range(RES):
                    wait_alone(pool, gathered[r], 16 * i, half_set)
            nc.gpsimd.tensor_copy(idx[:, :], x_ids[:, bass.ds(i, 1), :].rearrange("p o r -> p (o r)")).then_inc(idx_copied, 1)
            wait_alone(pool, idx_copied, i + 1, half_set)

        def gather(i, r):
            if not (isinstance(i, int) and i == 0):
                wait_alone(pool, cat_tr, RES * i + r + 1 - RES, half_set)
            nc.gpsimd.memset(cat[:, r, :], 0.0).then_inc(cat_zero, 1)
            wait_alone(pool, cat_zero, RES * i + r + 1, half_set)
            pool.indirect_dma_start(cat[:, r, :], None, table,
                                    bass.IndirectOffsetOnAxis(ap=idx[:, r:r + 1], axis=0),
                                    bounds_check=VOCAB - 1, oob_is_err=False).then_inc(gathered[r], 16)

        def group(i, ahead):
            if ahead:
                ids_of(i + 1)
            for r in range(RES):
                if ahead:
                    gather(i + 1, r)
                if r:
                    power_step(RES * i + r - 1, (r - 1) % 4, eps_done, rstd_done)
            power_step(RES * i + RES - 1, (RES - 1) % 4, eps_done, rstd_done)
            mids(i)

        def mids(i):
            for g in range(4):
                half = g % 2
                wait_alone(pool, mm_evac, 8 * i + g + 1, half_set)
                if g >= 2 or not (isinstance(i, int) and i == 0):
                    wait_alone(pool, sil_done, 4 * i + g - 1, half_set)
                nc.gpsimd.tensor_scalar(x_mid[:, g % 2, :, :], x_pad[:, g % 2, :, 1:SEQ + 1],
                                        vec[:, C_CONV + 3 * half + 1:C_CONV + 3 * half + 2], None,
                                        ALU.mult).then_inc(mid_done, 1)

        ids_of(0)
        for r in range(RES):
            gather(0, r)
        pool.wait_ge(rows_in, 32)
        steps = 0

        def link(ins):
            nonlocal steps
            steps += 1
            ins.then_inc(bias_step, 1)
            pool.wait_ge(bias_step, steps)

        link(nc.gpsimd.tensor_scalar(bias_e[:, :, :], bias_e[:, :, :], 0.25, None, ALU.mult))
        link(nc.gpsimd.tensor_scalar(row_in[:, 1, :], row_in[:, 1, :], 0.5, None, ALU.mult))
        link(nc.gpsimd.tensor_copy(row_in[:, 2, :], bias_e[:, RES - 1, :]))
        for e in range(RES - 1, -1, -1):
            before = bias_e[:, e - 1, :] if e else row_in[:, 2, :]
            link(nc.gpsimd.tensor_tensor(bias_e[:, e, :], bias_e[:, e, :], before, ALU.add))
            link(nc.gpsimd.tensor_tensor(bias_e[:, e, :], bias_e[:, e, :], row_in[:, 1, :], ALU.add))
        pool.wait_ge(half_set, 1)
        group(0, True)
        with pool.Fori(1, GROUPS - 1) as i:
            group(i, True)
        group(GROUPS - 1, False)

        pool.wait_ge(h_done, GROUPS * RES)
        pool.wait_ge(hn_done, GROUPS * RES)
        for g in range(GROUPS):
            nc.gpsimd.tensor_tensor(h_sb[:, g, :, :], h_sb[:, g, :, :],
                                    row_in[:, 0:1, :].broadcast_to([P, RES, D]), ALU.add).then_inc(h_biased, 1)

        pool.wait_ge(tp_hi_done, 32)
        pool.wait_ge(tp_lo_done, 32)
        pool.wait_ge(h_biased, GROUPS)

        def piece_in(n):
            pool.dma_start(stage[:, n % 4, :], w_b[:, n, :]).then_inc(stage_in[n % 4], 16)

        for n in range(4):
            piece_in(n)
        for n in range(7):
            hi = (w2_hi[:, :, :].rearrange("p k n -> p (k n)") if n == 0 else sw_hi[:, n - 1, :])
            lo = (w2_lo[:, :, :].rearrange("p k n -> p (k n)") if n == 0 else sw_lo[:, n - 1, :])
            pool.wait_ge(stage_in[n % 4], 16 * (n // 4 + 1))
            nc.gpsimd.tensor_copy(hi, stage[:, n % 4, :]).then_inc(w_hi_done, 1)
            pool.wait_ge(w_hi_done, n + 1)
            nc.gpsimd.tensor_tensor(lo, stage[:, n % 4, :], f32(hi), ALU.subtract).then_inc(w_lo_done, 1)
            if n + 4 < 7:
                pool.wait_ge(w_lo_done, n + 1)
                piece_in(n + 4)

        def expert_in(n, par):
            x = (n + (RES - 1)) & (RES - 1)
            pool.dma_start(stage[:, 2 * par:2 * par + 2, :],
                           w_e[bass.ds(x, 1), :, :, :].rearrange("o p k n -> (o p) k n")).then_inc(ex_in[par], 16)

        def expert_split(n, par, times):
            to = 1 - par
            wait_alone(pool, ex_in[par], 16 * times, half_set)
            nc.gpsimd.tensor_copy(ex_hi[to][:, :, :], stage[:, 2 * par:2 * par + 2, :]).then_inc(ex_hi_done, 1)
            wait_alone(pool, ex_hi_done, n + 1, half_set)
            nc.gpsimd.tensor_tensor(ex_lo[to][:, :, :], stage[:, 2 * par:2 * par + 2, :], f32(ex_hi[to][:, :, :]),
                                    ALU.subtract).then_inc(ex_done, 1)
            wait_alone(pool, ex_done, n + 1, half_set)

        pool.wait_ge(w_lo_done, 7)
        expert_in(0, 0)
        expert_in(1, 1)
        pool.wait_ge(ssm_done, NQ)
        expert_split(0, 0, 1)
        expert_in(2, 0)
        expert_split(1, 1, 1)

        def mixer_lo(e, g):
            n = GROUPS * e + g
            wait_alone(pool, zc_hi_done, n + 1, half_set)
            nc.gpsimd.tensor_tensor(zc_lo[:, g % 2, :, :], z_cols(e, g), f32(zc_hi[:, g % 2, :, :]),
                                    ALU.subtract).then_inc(zc_lo_done, 1)

        def mixer_bias(e, g):
            n = GROUPS * e + g
            wait_alone(pool, h2n_done, n + 1, half_set)
            at = h_sb[:, g, bass.ds(e, 1), :]
            nc.gpsimd.tensor_tensor(at, at, bias_e[:, bass.ds(e, 1), :], ALU.add).then_inc(h2_biased, 1)

        def mixer(e):
            mixer_lo(e, 0)
            mixer_lo(e, 1)
            for g in range(GROUPS):
                power_step(GROUPS * e + g, g, eps2_done, rstd2_done)
                mixer_bias(e, g)
                if g + 2 < GROUPS:
                    mixer_lo(e, g + 2)

        def slot(e, par, times):
            mixer(e + 1)
            if not (isinstance(e, int) and e + 3 > RES):
                expert_in(e + 3, 1 - par)
            wait_alone(pool, l2_done, UNITS * e + 2, half_set)
            expert_split(e + 2, par, times)

        mixer(0)
        slot(0, 0, 2)
        with pool.Fori(0, 2) as i:
            slot(2 * i + 1, 1, i + 2)
            slot(2 * i + 2, 0, i + 3)
        slot(5, 1, 4)
        slot(6, 0, 5)

    @block.scalar
    def _(act):
        act.wait_ge(vec_in, 16)
        nc.scalar.activation(abar[:, 0, :], vec[:, C_A:C_A + 32], ACT.Sigmoid).then_inc(abar_done, 1)
        act.wait_ge(wa_in, 16)
        nc.scalar.copy(proj_hi[:, :, :].rearrange("p k n -> p (k n)"), raw_a[:, 0:KC * D]).then_inc(wa_hi, 1)
        nc.scalar.copy(wv_hi[:, :, :, :].rearrange("p a k n -> p (a k n)"), raw_a[:, KC * D:]).then_inc(wa_hi, 1)

        def cat_hi(i, r):
            n = RES * i + r
            act.wait_ge(cat_tr, n + 1)
            nc.scalar.copy(catT_hi[:, r % 2, :, :].rearrange("p k n -> p (k n)"), ps[r % 2][:, 0:CAT]).then_inc(catT_hi_done, 1)

        def h_out(i, r):
            n = RES * i + r
            act.wait_ge(emb_done, n + 1)
            e = slot_of(r)
            nc.scalar.mul(h_sb[:, bass.ds(i, 1), e, :].rearrange("p o n -> p (o n)"), ps[2 + r % 2][:, 0:D],
                          EMB_SCALE).then_inc(h_done, 1)

        def turn_hi(i, what):
            n = turn_no(i, what)
            act.wait_ge(tp_filled, n + 1)
            bank = TP[turns(i).index(what) % 2]
            if what[0] == "hn":
                nc.scalar.copy(hnT_at(hnT_hi, what[1]), hn_bank(bank)).then_inc(tp_hi_done, 1)
            else:
                nc.scalar.copy(x_at(x_hi, i - 1, what[1]), x_bank(bank)).then_inc(tp_hi_done, 1)

        def x1_out(i, g):
            act.wait_ge(mm_done, 8 * i + g + 1)
            if g >= 2 or not (isinstance(i, int) and i == 0):
                act.wait_ge(conv_done, 4 * i + g - 1)
            half = g % 2
            nc.scalar.activation(x_pad[:, g % 2, :, 1:SEQ + 1], MM[g % 2][:, :].rearrange("p (b t) -> p b t", t=SEQ),
                                 ACT.Identity, bias=vec[:, C_W1B + half:C_W1B + half + 1]).then_inc(mm_evac, 1)

        def silu_x(i, g):
            act.wait_ge(conv_done, 4 * i + g + 1)
            nc.scalar.activation(x_sil[:, g, :, ::-1], x_mid[:, g % 2, :, :], ACT.Silu).then_inc(sil_done, 1)

        def v_out(i, g):
            act.wait_ge(mm_done, 8 * i + g + 1)
            k, half = (g - 4) // 2, g % 2
            at = v_sb[:, half, bass.ds(i * GTOK + k * BLK, BLK)]
            nc.scalar.activation(at, MM[g % 2][:, :], ACT.Silu, bias=vec[:, C_V1B + half:C_V1B + half + 1]).then_inc(mm_evac, 1)

        def group(i):
            for what in body_order(i):
                if what[0] == "cat":
                    cat_hi(i, what[1])
                elif what[0] == "emb":
                    h_out(i, what[1])
                else:
                    turn_hi(i, what)
            x1_out(i, 0)
            x1_out(i, 1)
            silu_x(i, 0)
            x1_out(i, 2)
            silu_x(i, 1)
            x1_out(i, 3)
            v_out(i, 4)
            silu_x(i, 2)
            v_out(i, 5)
            silu_x(i, 3)
            v_out(i, 6)
            v_out(i, 7)

        act.wait_ge(pad_zero, 1)
        group(0)
        with act.Fori(1, GROUPS) as i:
            group(i)
        for u in range(4):
            act.wait_ge(tp_filled, 28 + u + 1)
            nc.scalar.copy(x_at(x_hi, GROUPS - 1, u), x_bank(TP[u % 2])).then_inc(tp_hi_done, 1)
        act.wait_ge(tp_lo_done, 32)
        for q in range(0, NQ, 2):
            act.wait_ge(ssm_done, q + 1)
            nc.scalar.copy(y_at(q), y_bank(q)).then_inc(y_act, 1)

        def zc(e, g):
            n = GROUPS * e + g
            if g >= 2 or not (isinstance(e, int) and e == 0):
                act.wait_ge(w2_done, n - 1)
            else:
                act.wait_ge(z_done, 16)
            nc.scalar.copy(zc_hi[:, g % 2, :, :], z_cols(e, g)).then_inc(zc_hi_done, 1)

        def turn2_hi(e, par, g):
            act.wait_ge(tr2_done, GROUPS * e + g + 1)
            nc.scalar.copy(h2nT_hi[:, par, :, g * P:(g + 1) * P], tr2_bank()).then_inc(h2nT_hi_done, 1)

        def activate(e, n):
            kind, j, bank = PLAN[n]
            act.wait_ge(up_done, UNITS * e + n + 1)
            if kind == SHARED:
                nc.scalar.activation(act_out[:, n % 4, :], ps[bank][:, :], ACT.Silu,
                                     bias=vec[:, C_SB1 + j:C_SB1 + j + 1]).then_inc(act_done, 1)
            else:
                x = (e + (RES - 1)) & (RES - 1) if kind == OLD else e
                nc.scalar.activation(act_out[:, n % 4, :], ps[bank][:, :], ACT.Gelu,
                                     bias=vec[:, bass.ds(C_B1 + 2 * x + j, 1)]).then_inc(act_done, 1)

        def hidden_hi(e, n):
            kind, j, bank = PLAN[n]
            if kind == SHARED:
                act.wait_ge(gated, 4 * e + j + 1)
            else:
                act.wait_ge(act_done, UNITS * e + n + 1)
            nc.scalar.mul(hid_hi[:, n % 4, :], act_out[:, n % 4, :], 0.5 if kind == SHARED else 0.25).then_inc(hid_hi_done, 1)

        def slot(e, par, ahead, before):
            for n in range(UNITS):
                if ahead and n < 4:
                    zc(e + 1, n)
                if ahead and n >= 4:
                    turn2_hi(e + 1, 1 - par, n - 4)
                activate(e, n)
                if n or before:
                    hidden_hi(*((e, n - 1) if n else (e - 1, UNITS - 1)))

        for g in range(GROUPS):
            zc(0, g)
        for g in range(GROUPS):
            turn2_hi(0, 0, g)
        slot(0, 0, True, False)
        with act.Fori(0, 3) as i:
            slot(2 * i + 1, 1, True, True)
            slot(2 * i + 2, 0, True, True)
        slot(RES - 1, 1, False, True)
        hidden_hi(RES - 1, UNITS - 1)

    @block.vector
    def _(dve):
        nc.vector.memset(x_pad[:, :, :, :], 0.0).then_inc(pad_zero, 1)
        dve.wait_ge(wa_hi, 1)
        nc.vector.tensor_tensor(proj_lo[:, :, :].rearrange("p k n -> p (k n)"), raw_a[:, 0:KC * D],
                                f32(proj_hi[:, :, :].rearrange("p k n -> p (k n)")), ALU.subtract)
        dve.wait_ge(wa_hi, 2)
        nc.vector.tensor_tensor(wv_lo[:, :, :, :].rearrange("p a k n -> p (a k n)"), raw_a[:, KC * D:],
                                f32(wv_hi[:, :, :, :].rearrange("p a k n -> p (a k n)")), ALU.subtract).then_inc(wa_lo, 1)

        steps = 0

        def link(ins):
            nonlocal steps
            steps += 1
            ins.then_inc(k_step, 1)
            dve.wait_ge(k_step, steps)

        dve.wait_ge(abar_done, 1)
        link(nc.vector.memset(power[:, :, 0:1], 1.0))
        link(nc.vector.memset(k_row[:, :, :, :].rearrange("p h n w -> p (h n w)").bitcast(F32), 0.0))
        for k in range(7):
            n = 1 << k
            by = abar[:, k, :].rearrange("p (s o) -> p s o", o=1).broadcast_to([P, HALVES * STATES, n])
            link(nc.vector.tensor_tensor(power[:, :, n:2 * n], power[:, :, 0:n], by, ALU.mult))
            if k < 6:
                link(nc.vector.tensor_tensor(abar[:, k + 1, :], abar[:, k, :], abar[:, k, :], ALU.mult))
        link(nc.vector.tensor_tensor(bc[:, :], vec[:, C_B:C_B + 32], vec[:, C_C:C_C + 32], ALU.mult))
        by = bc[:, :].rearrange("p (s o) -> p s o", o=1).broadcast_to([P, HALVES * STATES, SEQ])
        link(nc.vector.tensor_tensor(power[:, :, :], power[:, :, :], by, ALU.mult))
        link(nc.vector.tensor_reduce(k_sum[:, :, :], power[:, :, :].rearrange("p (h s) t -> p h t s", h=HALVES),
                                     AX_X, ALU.add))
        link(nc.vector.tensor_tensor(k_sum[:, :, 0], k_sum[:, :, 0], vec[:, C_D:C_D + 2], ALU.add))
        link(nc.vector.tensor_copy(k_row[:, :, SEQ - 1:2 * SEQ - 1, 0], k_sum[:, :, :]))
        link(nc.vector.tensor_tensor(k_row[:, :, SEQ - 1:2 * SEQ - 1, 1], k_sum[:, :, :],
                                     k_row[:, :, SEQ - 1:2 * SEQ - 1, 0], ALU.subtract))
        assert steps == K_STEPS, steps

        def cat_lo(i, r):
            n = RES * i + r
            dve.wait_ge(catT_hi_done, n + 1)
            nc.vector.tensor_tensor(catT_lo[:, r % 2, :, :].rearrange("p k n -> p (k n)"), ps[r % 2][:, 0:CAT],
                                    f32(catT_hi[:, r % 2, :, :].rearrange("p k n -> p (k n)")),
                                    ALU.subtract).then_inc(catT_lo_done, 1)

        def norm(n, src, dst, m, s_stats, s_aggr, s_eps, s_rstd, s_out):
            nc.vector.bn_stats(stat[:, m, :], src).then_inc(s_stats, 1)
            wait_alone(dve, s_stats, n + 1, pad_zero)
            nc.vector.bn_aggr(mv[:, m, :], stat[:, m, :]).then_inc(s_aggr, 1)
            dve.wait_ge(s_aggr, n + 1)
            nc.vector.tensor_scalar(rstd[:, m:m + 1], mv[:, m, 1:2], EPS, None, ALU.add).then_inc(s_eps, 1)
            dve.wait_ge(s_rstd, n + 1)
            nc.vector.tensor_scalar(dst, src, mv[:, m, 0:1], rstd[:, m:m + 1], ALU.subtract, ALU.mult).then_inc(s_out, 1)

        def layer_norm(i, r):
            n = RES * i + r
            wait_alone(dve, h_done, n + 1, pad_zero)
            src = h_sb[:, bass.ds(i, 1), slot_of(r), :].rearrange("p o n -> p (o n)")
            norm(n, src, hn[:, r % 4, :], r % 4, stats_done, aggr_done, eps_done, rstd_done, hn_done)

        def turn_lo(i, what):
            n = turn_no(i, what)
            dve.wait_ge(tp_hi_done, n + 1)
            bank = TP[turns(i).index(what) % 2]
            if what[0] == "hn":
                nc.vector.tensor_tensor(hnT_at(hnT_lo, what[1]), hn_bank(bank), f32(hnT_at(hnT_hi, what[1])),
                                        ALU.subtract).then_inc(tp_lo_done, 1)
            else:
                nc.vector.tensor_tensor(x_at(x_lo, i - 1, what[1]), x_bank(bank), x_at(x_hi, i - 1, what[1]),
                                        ALU.subtract).then_inc(tp_lo_done, 1)

        def conv(i, g):
            half = g % 2
            c = C_CONV + 3 * half
            dve.wait_ge(mid_done, 4 * i + g + 1)
            nc.vector.scalar_tensor_tensor(x_mid[:, g % 2, :, :], x_pad[:, g % 2, :, 0:SEQ], vec[:, c:c + 1],
                                           x_mid[:, g % 2, :, :], ALU.mult, ALU.add).then_inc(conv_left, 1)
            dve.wait_ge(conv_left, 4 * i + g + 1)
            nc.vector.scalar_tensor_tensor(x_mid[:, g % 2, :, :], x_pad[:, g % 2, :, 2:SEQ + 2], vec[:, c + 2:c + 3],
                                           x_mid[:, g % 2, :, :], ALU.mult, ALU.add).then_inc(conv_done, 1)

        def group(i):
            for what in body_order(i):
                if what[0] == "cat":
                    cat_lo(i, what[1])
                elif what[0] == "emb":
                    layer_norm(i, what[1])
                else:
                    turn_lo(i, what)
            for g in range(4):
                conv(i, g)

        group(0)
        with dve.Fori(1, GROUPS) as i:
            group(i)
        for u in range(4):
            dve.wait_ge(tp_hi_done, 28 + u + 1)
            nc.vector.tensor_tensor(x_at(x_lo, GROUPS - 1, u), x_bank(TP[u % 2]), x_at(x_hi, GROUPS - 1, u),
                                    ALU.subtract).then_inc(tp_lo_done, 1)
        dve.wait_ge(tp_lo_done, 32)
        for q in range(1, NQ, 2):
            dve.wait_ge(ssm_done, q + 1)
            nc.vector.tensor_copy(y_at(q), y_bank(q)).then_inc(y_dve, 1)
        for u in range(16):
            k, half = u // 2, u % 2
            dve.wait_ge(yt_filled, u + 1)
            at = v_sb[:, half, k * BLK:(k + 1) * BLK]
            nc.vector.tensor_tensor(at, ps[4 + u % 4][:, :], at, ALU.mult).then_inc(z_done, 1)

        def mixer_out(e, g):
            n = GROUPS * e + g
            dve.wait_ge(w2_done, n + 1)
            at = h_sb[:, g, bass.ds(e, 1), :].rearrange("p o n -> p (o n)")
            nc.vector.tensor_tensor(at, ps[6][:, 0:D], at, ALU.add).then_inc(h2_done, 1)
            wait_alone(dve, h2_done, n + 1, pad_zero)
            norm(n, at, h2n[:, g, :], g, stats2_done, aggr2_done, eps2_done, rstd2_done, h2n_done)

        def turn2_lo(e, par, g):
            dve.wait_ge(h2nT_hi_done, GROUPS * e + g + 1)
            nc.vector.tensor_tensor(h2nT_lo[:, par, :, g * P:(g + 1) * P], tr2_bank(),
                                    f32(h2nT_hi[:, par, :, g * P:(g + 1) * P]), ALU.subtract).then_inc(h2nT_lo_done, 1)

        def gate(e, n):
            kind, j, bank = PLAN[n]
            if kind == SHARED:
                dve.wait_ge(act_done, UNITS * e + n + 1)
                nc.vector.scalar_tensor_tensor(act_out[:, n % 4, :], ps[bank + 1][:, :], vec[:, C_SB3 + j:C_SB3 + j + 1],
                                               act_out[:, n % 4, :], ALU.add, ALU.mult).then_inc(gated, 1)

        def hidden_lo(e, n):
            kind, j, bank = PLAN[n]
            dve.wait_ge(hid_hi_done, UNITS * e + n + 1)
            nc.vector.scalar_tensor_tensor(hid_lo[:, n % 4, :], act_out[:, n % 4, :], 0.5 if kind == SHARED else 0.25,
                                           f32(hid_hi[:, n % 4, :]), ALU.mult, ALU.subtract).then_inc(hid_lo_done, 1)

        def finish(e, par, times):
            dve.wait_ge(l2_done, UNITS * e + UNITS)
            dve.wait_ge(h2_biased, GROUPS * e + GROUPS)
            if times is not None:
                dve.wait_ge(stored[par], times)
            for g in range(GROUPS):
                nc.vector.tensor_tensor(o_sb[:, par, g, :], ps[4 + g // 2][:, (g % 2) * D:(g % 2 + 1) * D],
                                        h_sb[:, g, bass.ds(e, 1), :].rearrange("p o n -> p (o n)"),
                                        ALU.add).then_inc(o_done, 1)

        def slot(e, par, ahead, before, times=None):
            for n in range(UNITS):
                if n == 2 and before:
                    finish(e - 1, 1 - par, times)
                if ahead and 1 <= n <= 4:
                    mixer_out(e + 1, n - 1)
                if ahead and n >= 4:
                    turn2_lo(e + 1, 1 - par, n - 4)
                gate(e, n)
                if n or before:
                    hidden_lo(*((e, n - 1) if n else (e - 1, UNITS - 1)))

        for g in range(GROUPS):
            mixer_out(0, g)
        for g in range(GROUPS):
            turn2_lo(0, 0, g)
        slot(0, 0, True, False)
        slot(1, 1, True, True)
        slot(2, 0, True, True)
        with dve.Fori(0, 2) as i:
            slot(2 * i + 3, 1, True, True, 16 * i + 16)
            slot(2 * i + 4, 0, True, True, 16 * i + 16)
        slot(RES - 1, 1, False, True, 16 * 3)
        hidden_lo(RES - 1, UNITS - 1)
        finish(RES - 1, 1, 16 * 3)

    @block.tensor
    def _(pe):
        def three(out_, hi, lo, rhs_hi, rhs_lo, start, stop, shared_bank=False):
            kw = {"skip_group_check": True} if shared_bank else {}
            nc.tensor.matmul(out_, hi, rhs_hi, start=start, stop=False, **kw)
            nc.tensor.matmul(out_, hi, rhs_lo, start=False, stop=False, **kw)
            return nc.tensor.matmul(out_, lo, rhs_hi, start=False, stop=stop, **kw)

        def cat_turn(i, r):
            n = RES * i + r
            pe.wait_ge(gathered[r], 16 * (i + 1))
            if r >= 2 or not (isinstance(i, int) and i == 0):
                pe.wait_ge(catT_lo_done, n - 1)
            for k in range(KC):
                last = nc.tensor.transpose(ps[r % 2][:, k * P:(k + 1) * P], cat[:, r, k * P:(k + 1) * P], ident[:, :])
            last.then_inc(cat_tr, 1)

        def embed(i, r):
            n = RES * i + r
            pe.wait_ge(catT_lo_done, n + 1)
            if r >= 2 or not (isinstance(i, int) and i == 0):
                pe.wait_ge(h_done, n - 1)
            for k in range(KC):
                last = three(ps[2 + r % 2][:, 0:D], catT_hi[:, r % 2, k, :], catT_lo[:, r % 2, k, :],
                             proj_hi[:, k, :], proj_lo[:, k, :], k == 0, k == KC - 1)
            last.then_inc(emb_done, 1)

        def turn(i, what):
            n = turn_no(i, what)
            bank = TP[turns(i).index(what) % 2]
            if not (isinstance(n, int) and n < 2):
                pe.wait_ge(tp_lo_done, n - 1)
            if what[0] == "hn":
                pe.wait_ge(hn_done, RES * i + 2 * what[1] + 2)
                for r in range(2):
                    for half in range(HALVES):
                        at = (r * HALVES + half) * P
                        last = nc.tensor.transpose(bank[:, at:at + P], hn[:, (2 * what[1] + r) % 4, half * P:(half + 1) * P],
                                                   ident[:, :])
            else:
                pe.wait_ge(sil_done, 4 * i)
                last = x_turn(bank, what[1])
            last.then_inc(tp_filled, 1)

        def x_turn(bank, u):
            for b in range(4):
                last = nc.tensor.transpose(bank[:, b * P:(b + 1) * P], x_sil[:, u, b, :], ident[:, :])
            return last

        def project(i):
            pe.wait_ge(tp_lo_done, tp_before(i) + len(turns(i)))
            for g in range(8):
                which, k, half = g // 4, g % 4 // 2, g % 2
                if g >= 2 or not (isinstance(i, int) and i == 0):
                    pe.wait_ge(mm_evac, 8 * i + g - 1)
                for kk in range(HALVES):
                    cols = slice(k * BLK, (k + 1) * BLK)
                    last = three(MM[g % 2][:, :], wv_hi[:, which, kk, half * P:(half + 1) * P],
                                 wv_lo[:, which, kk, half * P:(half + 1) * P],
                                 hnT_hi[:, kk, cols], hnT_lo[:, kk, cols], kk == 0, kk == HALVES - 1)
                last.then_inc(mm_done, 1)

        def group(i):
            for what in body_order(i):
                if what[0] == "cat":
                    cat_turn(i, what[1])
                elif what[0] == "emb":
                    embed(i, what[1])
                else:
                    turn(i, what)
            project(i)

        pe.wait_ge(ident_step, 2)
        pe.wait_ge(wa_lo, 1)
        group(0)
        with pe.Fori(1, GROUPS) as i:
            group(i)
        for u in range(4):
            pe.wait_ge(tp_lo_done, 28 + u - 1)
            pe.wait_ge(sil_done, 16 - 3 + u)
            x_turn(TP[u % 2], u).then_inc(tp_filled, 1)

        pe.wait_ge(tp_lo_done, 32)
        for q in range(NQ):
            pe.wait_ge(toep_in[q % TRING], 16 * (q // TRING + 1))
            if q >= 4:
                pe.wait_ge(y_dve if q % 2 else y_act, (q - 4) // 2 + 1)
            for j in range(CH):
                c = q * CH + j
                at = ps[q % 4][:, j * BATCH:(j + 1) * BATCH]
                t_hi, t_lo = toep[:, q % TRING, j, :, 0], toep[:, q % TRING, j, :, 1]
                nc.tensor.matmul(at, t_hi, x_hi[:, c, :], start=True, stop=False)
                nc.tensor.matmul(at, t_hi, x_lo[:, c, :], start=False, stop=False)
                last = nc.tensor.matmul(at, t_lo, x_hi[:, c, :], start=False, stop=True)
            last.then_inc(ssm_done, 1)

        pe.wait_ge(y_act, NQ // 2)
        pe.wait_ge(y_dve, NQ // 2)
        for u in range(16):
            k, half = u // 2, u % 2
            if u >= 4:
                pe.wait_ge(z_done, u - 3)
            for b in range(4):
                last = nc.tensor.transpose(ps[4 + u % 4][:, b * P:(b + 1) * P],
                                           y_sb[:, 4 * k + b, half * P:(half + 1) * P], ident[:, :])
            last.then_inc(yt_filled, 1)

        def mixer_mm(e, g):
            n = GROUPS * e + g
            pe.wait_ge(zc_lo_done, n + 1)
            if g or not (isinstance(e, int) and e == 0):
                pe.wait_ge(h2_done, n)
            for k in range(HALVES):
                last = three(ps[6][:, 0:D], zc_hi[:, g % 2, k, :], zc_lo[:, g % 2, k, :],
                             w2_hi[:, k, :], w2_lo[:, k, :], k == 0, k == HALVES - 1)
            last.then_inc(w2_done, 1)

        def mixer_turn(e, g):
            n = GROUPS * e + g
            pe.wait_ge(h2n_done, n + 1)
            if g or not (isinstance(e, int) and e == 0):
                pe.wait_ge(h2nT_lo_done, n)
            for half in range(HALVES):
                last = nc.tensor.transpose(ps[7][:, half * P:(half + 1) * P], h2n[:, g, half * P:(half + 1) * P], ident[:, :])
            last.then_inc(tr2_done, 1)

        def free_banks(e, n):
            first = isinstance(e, int) and e == 0
            acts, gates = {0: (0, None), 1: (None, 0), 2: (0, None), 3: (2, None), 4: (3, 1), 5: (4, 2), 6: (5, None),
                           7: (None, 3)}[n]
            if acts is not None and not (first and acts == 0):
                pe.wait_ge(act_done, UNITS * e + acts)
            if gates is not None and not (first and gates == 0):
                pe.wait_ge(gated, 4 * e + gates)

        def hidden(e, par, n):
            kind, j, bank = PLAN[n]
            free_banks(e, n)
            new = par
            if kind == NEW and j == 0:
                pe.wait_ge(ex_done, e + 2)
            for which in range(2 if kind == SHARED else 1):
                for k in range(HALVES):
                    if kind == SHARED:
                        w_hi = sw_hi[:, 2 * which + k, j * P:(j + 1) * P]
                        w_lo = sw_lo[:, 2 * which + k, j * P:(j + 1) * P]
                    else:
                        m = new if kind == NEW else 1 - new
                        at = slice(k * HR + j * P, k * HR + (j + 1) * P)
                        w_hi, w_lo = ex_hi[m][:, 0, at], ex_lo[m][:, 0, at]
                    last = three(ps[bank + which][:, :], w_hi, w_lo, h2nT_hi[:, par, k, :], h2nT_lo[:, par, k, :],
                                 k == 0, k == HALVES - 1)
            last.then_inc(up_done, 1)

        def second(e, par, n):
            kind, j, bank = PLAN[n]
            pe.wait_ge(hid_lo_done, UNITS * e + n + 1)
            if n == 0 and not (isinstance(e, int) and e == 0):
                pe.wait_ge(o_done, GROUPS * e)
            if kind == SHARED:
                at = slice(j % 2 * D, (j % 2 + 1) * D)
                w_hi, w_lo = sw_hi[:, 4 + j // 2, at], sw_lo[:, 4 + j // 2, at]
            else:
                m = par if kind == NEW else 1 - par
                w_hi, w_lo = ex_hi[m][:, 1, j * D:(j + 1) * D], ex_lo[m][:, 1, j * D:(j + 1) * D]
            for g in range(GROUPS):
                last = three(ps[4 + g // 2][:, (g % 2) * D:(g % 2 + 1) * D], hid_hi[:, n % 4, g * P:(g + 1) * P],
                             hid_lo[:, n % 4, g * P:(g + 1) * P], w_hi, w_lo, n == 0 and g % 2 == 0, n == UNITS - 1,
                             shared_bank=True)
            last.then_inc(l2_done, 1)

        def slot(e, par, ahead, before):
            pe.wait_ge(h2nT_lo_done, GROUPS * e + GROUPS)
            for n in range(UNITS):
                hidden(e, par, n)
                if n >= 2:
                    second(e, par, n - 2)
                elif before:
                    second(e - 1, 1 - par, UNITS - 2 + n)
                if ahead and n < 4:
                    mixer_mm(e + 1, n)
                if ahead and 3 <= n <= 6:
                    mixer_turn(e + 1, n - 3)

        for g in range(GROUPS):
            mixer_mm(0, g)
        for g in range(GROUPS):
            mixer_turn(0, g)
        pe.wait_ge(w_lo_done, 7)
        pe.wait_ge(ex_done, 1)
        slot(0, 0, True, False)
        with pe.Fori(0, 3) as i:
            slot(2 * i + 1, 1, True, True)
            slot(2 * i + 2, 0, True, True)
        slot(RES - 1, 1, False, True)
        second(RES - 1, 1, UNITS - 2)
        second(RES - 1, 1, UNITS - 1)


def kernel(**inputs):
    import numpy as np
    import concourse.bacc as bacc
    from concourse import mybir as mb
    from concourse.bass_utils import run_bass_kernel_spmd as run

    a = {k: np.asarray(v) for k, v in inputs.items()}

    def tiles(w):
        k, n = w.shape
        return np.ascontiguousarray(w.reshape(k // P, P, n).transpose(1, 0, 2).reshape(P, -1))

    def cols(v):
        v = v.reshape(-1, P, v.size // v.shape[0] if v.ndim > 1 else 1)
        return v.transpose(1, 0, 2).reshape(P, -1)

    table = np.zeros((VOCAB, CAT), np.float32)
    proj = np.zeros((CAT, D), np.float32)
    row = col = 0
    for t in range(4):
        e, p = a[f"L0_tok_emb{t}"], a[f"L0_tok_proj{t}"]
        table[row:row + e.shape[0], col:col + e.shape[1]] = e
        proj[col:col + e.shape[1]] = p.T
        row, col = row + e.shape[0], col + e.shape[1]
    small = np.concatenate([cols(a["L0_attn_w1_b"]), cols(a["L0_attn_v1_b"]), cols(a["L0_attn_conv_w"].reshape(D, 3)),
                            cols(a["L0_attn_A"]), cols(a["L0_attn_B_ssm"]), cols(a["L0_attn_C_ssm"]),
                            cols(a["L0_attn_D_ssm"]), cols(a["L0_ffn_sb1"]), cols(a["L0_ffn_sb3"]),
                            cols(a["L0_ffn_b1"].reshape(-1))], axis=1)
    rows = np.concatenate([a["L0_attn_w2_b"], a["L0_ffn_sb2"], a["L0_ffn_b2"].reshape(-1)])
    w_a = np.concatenate([tiles(proj), tiles(a["L0_attn_w1_w"].T), tiles(a["L0_attn_v1_w"].T)], axis=1)
    w_b = np.concatenate([tiles(a["L0_attn_w2_w"].T), tiles(a["L0_ffn_sw1"]), tiles(a["L0_ffn_sw3"]),
                          tiles(a["L0_ffn_sw2"])], axis=1).reshape(P, 7, BLK)
    w_e = np.stack([np.stack([tiles(a["L0_ffn_w1"][e]), tiles(a["L0_ffn_w2"][e])], axis=1) for e in range(RES)])
    arrays = {"ids": a["x"].reshape(-1), "table": table, "small": small, "rows": rows, "w_a": w_a, "w_b": w_b, "w_e": w_e}
    arrays = {k: np.ascontiguousarray(v) for k, v in arrays.items()}

    nc = bacc.Bacc("TRN2", target_bir_lowering=False, num_devices=1)
    args = [nc.dram_tensor(f"{k}_dram", v.shape, mb.dt.from_np(v.dtype), kind="ExternalInput").ap()
            for k, v in arrays.items()]
    scratch = nc.dram_tensor("kernel_rows_dram", (D, YLEN), F32, kind="Internal").ap()
    out = nc.dram_tensor("out_dram", (BATCH * SEQ, D), F32, kind="ExternalOutput").ap()
    tower(nc, *args, scratch, out)
    r = run(nc, [{f"{k}_dram": v for k, v in arrays.items()}], core_ids=[0])
    return r.results[0]["out_dram"].reshape(BATCH, SEQ, D)
```

```python
from contextlib import ExitStack

import concourse.bass as bass
from concourse import mybir

F32 = mybir.dt.float32
F32R = mybir.dt.float32r
F16 = mybir.dt.float16
I32 = mybir.dt.int32
ALU = mybir.AluOpType
ACT = mybir.ActivationFunctionType
AX_X = mybir.AxisListType.X

P = 128
BATCH, SEQ, D = 32, 128, 256
VOCAB = 32000
CAT = 384
KC = CAT // P
HALVES = D // P
RES = 8
GROUPS = BATCH * SEQ // (P * RES)
GTOK = P * RES
BLK = 512
STATES = 16
HS = 512
HR = 256
UNITS = 8
EMB_SCALE = float(D) ** 0.5
EPS = 1e-5
CH = 16
NQ = D // CH
TRIGHT, TLEFT = 4, 3
TRING = TRIGHT + TLEFT
YLEN = 256
PAIRS = CH // 2
HALF = SEQ // 2

C_W1B, C_V1B, C_CONV = 0, 2, 4
C_A, C_B, C_C, C_D = 10, 42, 74, 106
C_SB1, C_SB3, C_B1 = 108, 112, 116
NSMALL = 132

OLD, SHARED, NEW = range(3)
PLAN = [(OLD, 0, 0), (OLD, 1, 1), (SHARED, 0, 2), (SHARED, 1, 0), (SHARED, 2, 2), (SHARED, 3, 0), (NEW, 0, 2), (NEW, 1, 3)]


def slot_of(r):
    return 3 * r % RES


def tower(nc, ids, table, small, rows, w_a, w_b, w_e, kernel_rows, h_rows, out):
    ctx = ExitStack()
    with ctx:
        _tower(nc, ctx, ids, table, small, rows, w_a, w_b, w_e, kernel_rows, h_rows, out)


def _tower(nc, ctx, ids, table, small, rows, w_a, w_b, w_e, kernel_rows, h_rows, out):
    def sem(name):
        return ctx.enter_context(nc.semaphore(name))

    def sb(stack, name, shape, dt, side):
        return stack.enter_context(nc.sbuf_tensor(name, shape, dt, side=side))

    R, L = "right", "left"
    v_sb = sb(ctx, "v_sb", [P, HALVES, BATCH * SEQ], F32, R)
    w2_hi = sb(ctx, "w2_hi", [P, HALVES, D], F32R, R)
    w2_lo = sb(ctx, "w2_lo", [P, HALVES, D], F32R, R)
    bias_e = sb(ctx, "bias_e", [P, RES, D], F32, R)
    bias_row = sb(ctx, "bias_row", [P, 2, D], F32, R)
    w2_bias = bias_row[:, 0:1, :]
    vec = sb(ctx, "vec", [P, NSMALL], F32, R)
    ident = sb(ctx, "ident", [P, P], F32, R)
    stat = sb(ctx, "stat", [P, 4, 6], F32, R)
    mv = sb(ctx, "mv", [P, 4, 2], F32, R)
    rstd = sb(ctx, "rstd", [P, 4], F32, R)
    minus_half = sb(ctx, "minus_half", [P, 1], F32, R)
    zero = sb(ctx, "zero", [P, 1], F32, R)
    warm_out = sb(ctx, "warm_out", [P, 2], F32, R)
    mid_bias = sb(ctx, "mid_bias", [P, HALVES], F32, R)

    ssm_mem = ExitStack()
    x_hi = sb(ssm_mem, "x_hi", [P, D, BATCH], F16, R)
    x_lo = sb(ssm_mem, "x_lo", [P, D, BATCH], F16, R)
    toep_r = sb(ssm_mem, "toep_r", [P, TRIGHT, PAIRS, SEQ, 2, 2], F16, R)
    flat = toep_r[:, :, :, :, :, :].rearrange("p a j t c w -> p (a j t c w)").bitcast(F32)
    power = flat[:, 0:HALVES * STATES * SEQ].rearrange("p (s t) -> p s t", t=SEQ)
    raw_at = HALVES * STATES * SEQ
    raw_a = flat[:, raw_at:raw_at + (KC + 4) * D]
    k_sum = flat[:, raw_at + (KC + 4) * D:raw_at + (KC + 5) * D].rearrange("p (h t) -> p h t", t=SEQ)

    mem_a = ExitStack()
    x_ids = sb(mem_a, "x_ids", [P, GROUPS, RES], I32, L)
    idx = sb(mem_a, "idx", [P, RES], I32, L)
    cat = sb(mem_a, "cat", [P, RES, CAT], F32, L)
    catT_hi = sb(mem_a, "catT_hi", [P, 2, KC, P], F32R, L)
    catT_lo = sb(mem_a, "catT_lo", [P, 2, KC, P], F32R, L)
    hn = sb(mem_a, "hn", [P, 4, D], F32, L)
    proj_hi = sb(mem_a, "proj_hi", [P, KC, D], F32R, L)
    proj_lo = sb(mem_a, "proj_lo", [P, KC, D], F32R, L)
    h_ring = sb(mem_a, "h_ring", [P, 4, D], F32, L)
    hnT_hi = sb(mem_a, "hnT_hi", [P, 2, HALVES, GTOK], F32R, L)
    hnT_lo = sb(mem_a, "hnT_lo", [P, 2, HALVES, GTOK], F32R, L)
    x_pad = sb(mem_a, "x_pad", [P, 2, 4, SEQ + 2], F32, L)
    x_mid = sb(mem_a, "x_mid", [P, 2, 4, SEQ], F32, L)
    x_sil = sb(mem_a, "x_sil", [P, 4, 4, SEQ], F32, L)
    wv_hi = sb(mem_a, "wv_hi", [P, 2, HALVES, D], F32R, L)
    wv_lo = sb(mem_a, "wv_lo", [P, 2, HALVES, D], F32R, L)
    abar = sb(mem_a, "abar", [P, 7, HALVES * STATES], F32, L)
    k_row = sb(mem_a, "k_row", [P, YLEN, 2, 2], F16, L)
    mem_a.close()

    toep_l = sb(ctx, "toep_l", [P, TLEFT, PAIRS, SEQ, 2, 2], F16, L)
    sw_hi = sb(ctx, "sw_hi", [P, 6, BLK], F32R, L)
    sw_lo = sb(ctx, "sw_lo", [P, 6, BLK], F32R, L)
    ex0_hi = sb(ctx, "ex0_hi", [P, 2, BLK], F32R, L)
    ex0_lo = sb(ctx, "ex0_lo", [P, 2, BLK], F32R, L)
    stage = sb(ctx, "stage", [P, 4, BLK], F32, L)
    mem_y = ExitStack()
    y_sb = sb(mem_y, "y_sb", [P, BATCH, D], F32, L)
    mem_y.close()
    ssm_mem.close()

    ex1_hi = sb(ctx, "ex1_hi", [P, 2, BLK], F32R, R)
    ex1_lo = sb(ctx, "ex1_lo", [P, 2, BLK], F32R, R)
    zc_hi = sb(ctx, "zc_hi", [P, 2, HALVES, P], F32R, R)
    zc_lo = sb(ctx, "zc_lo", [P, 2, HALVES, P], F32R, R)
    h_in = sb(ctx, "h_in", [P, 2, GROUPS, D], F32, R)
    h2_sb = sb(ctx, "h2_sb", [P, 2, GROUPS, D], F32, R)
    h2n = sb(ctx, "h2n", [P, 4, D], F32, R)
    h2nT_hi = sb(ctx, "h2nT_hi", [P, 2, HALVES, BLK], F32R, R)
    h2nT_lo = sb(ctx, "h2nT_lo", [P, 2, HALVES, BLK], F32R, R)
    hid_hi = sb(ctx, "hid_hi", [P, 4, BLK], F32R, R)
    hid_lo = sb(ctx, "hid_lo", [P, 4, BLK], F32R, R)
    act_out = sb(ctx, "act_out", [P, 4, BLK], F32, R)
    o_sb = sb(ctx, "o_sb", [P, 2, GROUPS, D], F32, R)
    ex_hi, ex_lo = [ex0_hi, ex1_hi], [ex0_lo, ex1_lo]

    ps = [ctx.enter_context(nc.psum_tensor(f"ps{i}", [P, BLK], F32)) for i in range(8)]
    CATP, EMBP, HNP, XP, MM = ps[0:2], ps[2:4], ps[4], ps[5], ps[6:8]

    ids_in = sem("ids_in")
    vec_in = sem("vec_in")
    wa_in = sem("wa_in")
    rows_in = sem("rows_in")
    ident_step = sem("ident_step")
    half_set = sem("half_set")
    pad_zero = sem("pad_zero")
    row_zero = sem("row_zero")
    wa_hi = sem("wa_hi")
    wa_lo = sem("wa_lo")
    abar_done = sem("abar_done")
    k_step = sem("k_step")
    k_out = sem("k_out")
    bias_step = sem("bias_step")
    idx_copied = sem("idx_copied")
    cat_zero = sem("cat_zero")
    gathered = [sem(f"gathered{r}") for r in range(RES)]
    cat_tr = sem("cat_tr")
    catT_hi_done = sem("catT_hi_done")
    catT_lo_done = sem("catT_lo_done")
    emb_done = sem("emb_done")
    h_done = sem("h_done")
    h_stored = [sem(f"h_stored{s}") for s in range(4)]
    stats_done = sem("stats_done")
    aggr_done = sem("aggr_done")
    eps_done = sem("eps_done")
    rstd_done = sem("rstd_done")
    hn_done = sem("hn_done")
    hn_turned = sem("hn_turned")
    hnT_hi_done = sem("hnT_hi_done")
    hnT_lo_done = sem("hnT_lo_done")
    mm_done = sem("mm_done")
    mm_evac = sem("mm_evac")
    mid_done = sem("mid_done")
    conv_left = sem("conv_left")
    conv_done = sem("conv_done")
    sil_done = sem("sil_done")
    x_turned = sem("x_turned")
    x_hi_done = sem("x_hi_done")
    x_lo_done = sem("x_lo_done")
    toep_in = [sem(f"toep_in{s}") for s in range(TRING)]
    ssm_done = sem("ssm_done")
    y_act = sem("y_act")
    y_dve = sem("y_dve")
    yt_filled = sem("yt_filled")
    z_done = sem("z_done")
    stage_in = [sem(f"stage_in{s}") for s in range(4)]
    w_hi_done = sem("w_hi_done")
    w_lo_done = sem("w_lo_done")
    ex_in = [sem(f"ex_in{s}") for s in range(2)]
    ex_hi_done = sem("ex_hi_done")
    ex_done = sem("ex_done")
    h_back = [sem(f"h_back{s}") for s in range(2)]
    h_biased = sem("h_biased")
    zc_hi_done = sem("zc_hi_done")
    zc_lo_done = sem("zc_lo_done")
    w2_done = sem("w2_done")
    h2_done = sem("h2_done")
    stats2_done = sem("stats2_done")
    aggr2_done = sem("aggr2_done")
    eps2_done = sem("eps2_done")
    rstd2_done = sem("rstd2_done")
    h2n_done = sem("h2n_done")
    h2_biased = sem("h2_biased")
    tr2_done = sem("tr2_done")
    h2nT_hi_done = sem("h2nT_hi_done")
    h2nT_lo_done = sem("h2nT_lo_done")
    up_done = sem("up_done")
    act_done = sem("act_done")
    gated = sem("gated")
    hid_hi_done = sem("hid_hi_done")
    hid_lo_done = sem("hid_lo_done")
    l2_done = sem("l2_done")
    o_done = sem("o_done")
    stored = [sem(f"stored{s}") for s in range(2)]

    def f32(ap):
        return ap.bitcast(F32)

    def need(eng, signal, count, passed=None, value=1):
        if isinstance(count, int):
            if count > 0:
                eng.wait_ge(signal, count)
            return
        if passed is not None:
            eng.compute_val(count)
            eng.wait_ge(passed, value)
        eng.wait_ge(signal, count)

    def phase_a(i):
        def there(back):
            return 0 <= i - back < GROUPS if isinstance(i, int) else True
        out_ = []

        def add(name, back, index):
            if there(back):
                out_.append((name, i - back if back else i, index))

        for r in range(RES):
            add("cat", 0, r)
            if r < 4:
                add("out", 2, 4 + r)
            else:
                add("out", 1, r - 4)
            add("emb", 0, r - 1) if r else add("emb", 1, RES - 1)
            add("stats", 0, r - 1) if r else add("stats", 1, RES - 1)
            add("norm", 0, r - 2) if r >= 2 else add("norm", 1, RES - 2 + r)
            add("aggr", 0, r - 1) if r else add("aggr", 1, RES - 1)
            if r >= 4:
                add("conv_left", 1, r - 4)
            add("eps", 0, r - 1) if r else add("eps", 1, RES - 1)
            if r >= 4:
                add("conv_right", 1, r - 4)
            if r in (0, 2):
                add("hn", 1, 2 + r // 2)
            if r in (4, 6):
                add("hn", 0, (r - 4) // 2)
            if r < 2:
                add("x", 2, 2 + r)
            if r >= 6:
                add("x", 1, r - 6)
            if r >= 5:
                add("silu", 1, r - 5)
            if r == 0:
                add("silu", 2, 3)
            add("mm", 2, 5 + r) if r < 3 else add("mm", 1, r - 3)
        return out_

    def run_phase_a(eng, tasks):
        def body(i):
            for name, group, index in phase_a(i):
                if name in tasks:
                    tasks[name](group, index)

        body(0)
        body(1)
        with eng.Fori(2, GROUPS) as i:
            body(i)
        body(GROUPS)
        body(GROUPS + 1)

    K_STEPS = 1 + 7 + 6 + 4 + 3
    BIAS_STEPS = 3 + 2 * RES

    def hn_bank():
        return HNP[:, :].rearrange("c (r h p) -> c h p r", r=2, h=HALVES)

    def hnT_at(t, i, pair):
        v = t[:, bass.ds(i & 1, 1), :, :].rearrange("c o h (p r) -> c (o h) p r", r=RES)
        return v[:, :, :, 2 * pair:2 * pair + 2]

    def x_bank():
        return XP[:, :].rearrange("u (b c) -> u b c", b=4)

    def x_at(t, i, u):
        k, half = u // 2, u % 2
        v = t[:, half * P:(half + 1) * P, :].rearrange("u c b -> u b c")
        return v[:, bass.ds(8 * i + 4 * k, 4), :]

    def toep(q):
        slot = q % TRING
        return toep_r[:, slot, :, :, :, :] if slot < TRIGHT else toep_l[:, slot - TRIGHT, :, :, :, :]

    def y_bank(q):
        return ps[q % 4][:, :].rearrange("t (c b) -> t c b", c=CH)

    def y_at(q):
        return y_sb[:, :, q * CH:(q + 1) * CH].rearrange("t b c -> t c b")

    def yt_bank(u):
        return ps[4 * (1 - u // 8) + u % 4]

    def tr2_bank():
        return ps[7][:, 0:D].rearrange("c (h p) -> c h p", h=HALVES)

    def z_cols(e, g):
        r = (3 * e) & (RES - 1)
        v = v_sb[:, :, g * GTOK:(g + 1) * GTOK].rearrange("c h (p r) -> c h r p", r=RES)
        return v[:, :, bass.ds(r, 1), :].rearrange("c h o p -> c h (o p)")

    PIECES = [(stage[:, n % 4, :], sw_hi[:, n - 1, :] if n else w2_hi[:, :, :].rearrange("p k n -> p (k n)"),
               sw_lo[:, n - 1, :] if n else w2_lo[:, :, :].rearrange("p k n -> p (k n)"), stage_in[n % 4],
               16 * (n // 4 + 1)) for n in range(7)]
    PIECES += [(stage[:, 2:4, :], ex0_hi[:, :, :], ex0_lo[:, :, :], ex_in[1], 16),
               (stage[:, 0:2, :], ex1_hi[:, :, :], ex1_lo[:, :, :], ex_in[0], 16)]

    block = ctx.enter_context(nc.Block())

    @block.sync
    def _(sp):
        sp.dma_start(x_ids[:, :, :], ids.rearrange("(g p r) -> p g r", p=P, r=RES)).then_inc(ids_in, 16)
        sp.dma_start(vec[:, :], small).then_inc(vec_in, 16)
        sp.dma_start(raw_a, w_a).then_inc(wa_in, 16)
        sp.dma_start(bias_row[:, 0:1, :], bass.AP(rows.tensor, D, [[0, P], [D, 1], [1, D]])).then_inc(rows_in, 16)
        sp.dma_start(bias_e[:, :, :], bass.AP(rows.tensor, 2 * D, [[0, P], [D, RES], [1, D]])).then_inc(rows_in, 16)

        def h_store(i, r):
            need(sp, h_done, RES * i + r + 1, ids_in, 16)
            sp.dma_start(h_rows[slot_of(r), :, bass.ds(i, 1), :].rearrange("p o c -> p (o c)"),
                         h_ring[:, r % 4, :]).then_inc(h_stored[r % 4], 16)

        def toep_part(q, first, n, t):
            src = bass.AP(kernel_rows.tensor, q * PAIRS * 2 * YLEN + 2 * (first + t),
                          [[2, n], [2 * YLEN, PAIRS], [1, 2 * (SEQ - t)]])
            dst = toep(q)[first:first + n, :, t:, :, :].rearrange("p j t c w -> p j (t c w)").bitcast(F32)
            sp.dma_start(dst, src).then_inc(toep_in[q % TRING], 16)

        def toep_load(q):
            if q < TRING:
                toep_part(q, 0, P, 0)
            else:
                toep_part(q, 0, HALF, HALF)
                toep_part(q, HALF, HALF, 0)

        for r in range(RES):
            h_store(0, r)
        sp.wait_ge(k_step, K_STEPS)
        sp.dma_start(kernel_rows, k_row[:, :, :, :].rearrange("p n c w -> p (n c w)").bitcast(F32)).then_inc(k_out, 16)
        sp.wait_ge(k_out, 16)
        sp.wait_ge(wa_lo, 2)
        for r in range(RES):
            h_store(1, r)
            if r % 2:
                toep_load(r // 2)
        with sp.Fori(2, GROUPS) as i:
            for r in range(RES):
                h_store(i, r)
        sp.wait_ge(hn_turned, 4 * GROUPS)
        sp.wait_ge(catT_lo_done, RES * GROUPS)
        for s in range(4):
            sp.wait_ge(h_stored[s], 16 * 2 * GROUPS)
        for q in range(TRIGHT, NQ):
            if q >= TRING:
                sp.wait_ge(ssm_done, q - TRING + 1)
            toep_load(q)

        def h_load(e, par):
            sp.dma_start(h_in[:, par, :, :],
                         h_rows[bass.ds(e, 1), :, :, :].rearrange("o p g c -> (o p) g c")).then_inc(h_back[par], 16)

        def store(e, par):
            need(sp, o_done, GROUPS * e + GROUPS, ids_in, 16)
            r = (3 * e) & (RES - 1)
            dst = out.rearrange("(g p r) c -> r p g c", p=P, r=RES)
            sp.dma_start(dst[bass.ds(r, 1), :, :, :].rearrange("o p g c -> (o p) g c"),
                         o_sb[:, par, :, :]).then_inc(stored[par], 16)

        sp.wait_ge(bias_step, BIAS_STEPS)
        sp.dma_start(w2_bias, bass.AP(rows.tensor, 0, [[0, P], [D, 1], [1, D]])).then_inc(rows_in, 16)
        sp.wait_ge(ssm_done, NQ)
        h_load(0, 0)
        h_load(1, 1)
        sp.wait_ge(h2_done, GROUPS)
        h_load(2, 0)
        store(0, 0)
        h_load(3, 1)
        with sp.Fori(0, 2) as i:
            store(2 * i + 1, 1)
            h_load(2 * i + 4, 0)
            store(2 * i + 2, 0)
            h_load(2 * i + 5, 1)
        store(RES - 3, 1)
        store(RES - 2, 0)
        store(RES - 1, 1)
        sp.wait_ge(stored[0], 16 * RES // 2)
        sp.wait_ge(stored[1], 16 * RES // 2)

    @block.gpsimd
    def _(pool):
        nc.gpsimd.memset(ident[:, :], 0.0).then_inc(ident_step, 1)
        nc.gpsimd.memset(zero[:, :], 0.0)
        nc.gpsimd.memset(minus_half[:, :], -0.5).then_inc(half_set, 1)
        nc.gpsimd.memset(cat[:, :, :], 0.0).then_inc(cat_zero, RES)

        def gather(i, r):
            n = RES * i + r + 1
            if not isinstance(i, int) or i:
                need(pool, catT_lo_done, n - RES, half_set)
                nc.gpsimd.memset(cat[:, r, :], 0.0).then_inc(cat_zero, 1)
            nc.gpsimd.tensor_copy(idx[:, r:r + 1], x_ids[:, bass.ds(i, 1), r:r + 1].rearrange("p o r -> p (o r)")
                                  ).then_inc(idx_copied, 1)
            need(pool, idx_copied, n, half_set)
            need(pool, cat_zero, n, half_set)
            pool.indirect_dma_start(cat[:, r, :], None, table,
                                    bass.IndirectOffsetOnAxis(ap=idx[:, r:r + 1], axis=0),
                                    bounds_check=VOCAB - 1, oob_is_err=False).then_inc(gathered[r], 16)

        def power_step(n, m, s_eps, s_rstd):
            need(pool, s_eps, n + 1, half_set)
            nc.gpsimd.tensor_tensor(rstd[:, m:m + 1], rstd[:, m:m + 1], minus_half[:, :], ALU.pow).then_inc(s_rstd, 1)

        def group(i, ahead):
            for r in range(RES):
                if r or not isinstance(i, int) or i:
                    power_step(RES * i + r - 1, (r - 1) % 4, eps_done, rstd_done)
                if ahead:
                    gather(i + 1, r)

        pool.wait_ge(ids_in, 16)
        gather(0, 0)
        pool.wait_ge(ident_step, 1)
        nc.gpsimd.affine_select(out=ident[:, :], in_=ident[:, :], compare_op=ALU.not_equal, fill=1.0, base=0,
                                pattern=[[-1, P]], channel_multiplier=1).then_inc(ident_step, 1)
        for r in range(1, RES):
            gather(0, r)
        group(0, True)
        with pool.Fori(1, GROUPS - 1) as i:
            group(i, True)
        group(GROUPS - 1, False)
        power_step(RES * GROUPS - 1, (RES - 1) % 4, eps_done, rstd_done)

        def piece_in(n):
            pool.dma_start(stage[:, n % 4, :], w_b[:, n, :]).then_inc(stage_in[n % 4], 16)

        def expert_in(n, par):
            x = (n + (RES - 1)) & (RES - 1)
            pool.dma_start(stage[:, 2 * par:2 * par + 2, :],
                           w_e[bass.ds(x, 1), :, :, :].rearrange("o p k n -> (o p) k n")).then_inc(ex_in[par], 16)

        steps = 0

        def link(ins):
            nonlocal steps
            steps += 1
            ins.then_inc(bias_step, 1)
            pool.wait_ge(bias_step, steps)

        def slot_bias(e):
            before = bias_e[:, e - 1, :] if e else bias_row[:, 1, :]
            link(nc.gpsimd.tensor_tensor(bias_e[:, e, :], bias_e[:, e, :], before, ALU.add))
            link(nc.gpsimd.tensor_tensor(bias_e[:, e, :], bias_e[:, e, :], bias_row[:, 0, :], ALU.add))

        pool.wait_ge(ssm_done, 1)
        for n in range(4):
            piece_in(n)
        pool.wait_ge(rows_in, 32)
        link(nc.gpsimd.tensor_scalar(bias_e[:, :, :], bias_e[:, :, :], 0.25, None, ALU.mult))
        link(nc.gpsimd.tensor_scalar(bias_row[:, 0, :], bias_row[:, 0, :], 0.5, None, ALU.mult))
        link(nc.gpsimd.tensor_copy(bias_row[:, 1, :], bias_e[:, RES - 1, :]))
        for n in range(4, 7):
            pool.wait_ge(w_lo_done, n - 3)
            piece_in(n)
            for e in {4: (7, 6, 5), 5: (4, 3, 2), 6: (1, 0)}[n]:
                slot_bias(e)
        assert steps == BIAS_STEPS
        pool.wait_ge(w_lo_done, 6)
        expert_in(0, 0)
        pool.wait_ge(w_lo_done, 7)
        expert_in(1, 1)

        def expert_split(n, par, times):
            to = 1 - par
            need(pool, ex_in[par], 16 * times, half_set)
            nc.gpsimd.tensor_copy(ex_hi[to][:, :, :], stage[:, 2 * par:2 * par + 2, :]).then_inc(ex_hi_done, 1)
            need(pool, ex_hi_done, n - 1, half_set)
            nc.gpsimd.tensor_tensor(ex_lo[to][:, :, :], stage[:, 2 * par:2 * par + 2, :], f32(ex_hi[to][:, :, :]),
                                    ALU.subtract).then_inc(ex_done, 1)
            need(pool, ex_done, n - 1, half_set)

        def mixer_lo(e, g):
            need(pool, zc_hi_done, GROUPS * e + g + 1, half_set)
            nc.gpsimd.tensor_tensor(zc_lo[:, g % 2, :, :], z_cols(e, g), f32(zc_hi[:, g % 2, :, :]),
                                    ALU.subtract).then_inc(zc_lo_done, 1)

        def mixer_bias(e, par, g):
            need(pool, h2n_done, GROUPS * e + g + 1, half_set)
            at = h2_sb[:, par, g, :]
            nc.gpsimd.tensor_tensor(at, at, bias_e[:, bass.ds(e, 1), :].rearrange("p o c -> p (o c)"),
                                    ALU.add).then_inc(h2_biased, 1)

        def mixer(e, par):
            mixer_lo(e, 0)
            mixer_lo(e, 1)
            for g in range(GROUPS):
                power_step(GROUPS * e + g, g, eps2_done, rstd2_done)
                mixer_bias(e, par, g)
                if g + 2 < GROUPS:
                    mixer_lo(e, g + 2)

        def add_w2_bias(par, times):
            need(pool, h_back[par], 16 * times, half_set)
            at = h_in[:, par, :, :]
            nc.gpsimd.tensor_tensor(at, at, w2_bias[:, :, :].broadcast_to([P, GROUPS, D]), ALU.add).then_inc(h_biased, 1)

        def slot(e, par, times, load=True, bias=True):
            mixer(e + 1, 1 - par)
            if load:
                expert_in(e + 3, 1 - par)
            need(pool, l2_done, UNITS * e + 2, half_set)
            expert_split(e + 2, par, times)
            if bias:
                add_w2_bias(par, times)

        mixer_lo(0, 0)
        mixer_lo(0, 1)
        pool.wait_ge(rows_in, 48)
        add_w2_bias(0, 1)
        for g in range(GROUPS):
            power_step(g, g, eps2_done, rstd2_done)
            if g + 2 < GROUPS:
                mixer_lo(0, g + 2)
        for g in range(GROUPS):
            mixer_bias(0, 0, g)
        add_w2_bias(1, 1)
        pool.wait_ge(w_lo_done, len(PIECES))
        expert_in(2, 0)
        slot(0, 0, 2)
        with pool.Fori(0, 2) as i:
            slot(2 * i + 1, 1, i + 2)
            slot(2 * i + 2, 0, i + 3)
        slot(5, 1, 4)
        slot(6, 0, 5, load=False, bias=False)

    @block.scalar
    def _(act):
        act.wait_ge(vec_in, 16)
        nc.scalar.activation(abar[:, 0, :], vec[:, C_A:C_A + 32], ACT.Sigmoid).then_inc(abar_done, 1)
        act.wait_ge(wa_in, 16)
        nc.scalar.copy(proj_hi[:, :, :].rearrange("p k n -> p (k n)"), raw_a[:, 0:KC * D]).then_inc(wa_hi, 1)
        nc.scalar.copy(wv_hi[:, :, :, :].rearrange("p a k n -> p (a k n)"), raw_a[:, KC * D:]).then_inc(wa_hi, 1)

        def cat_hi(i, r):
            n = RES * i + r
            need(act, cat_tr, n + 1)
            nc.scalar.copy(catT_hi[:, r % 2, :, :].rearrange("p k n -> p (k n)"), CATP[r % 2][:, 0:CAT]).then_inc(catT_hi_done, 1)

        def h_out(i, r):
            n = RES * i + r
            need(act, emb_done, n + 1)
            uses = 2 * i + r // 4
            need(act, h_stored[r % 4], 16 * uses)
            need(act, hn_done, n - 3)
            nc.scalar.mul(h_ring[:, r % 4, :], EMBP[r % 2][:, 0:D], EMB_SCALE).then_inc(h_done, 1)

        def hn_hi(i, pair):
            need(act, hn_turned, 4 * i + pair + 1)
            nc.scalar.copy(hnT_at(hnT_hi, i, pair), hn_bank()).then_inc(hnT_hi_done, 1)

        def x_hi_part(i, u):
            need(act, x_turned, 4 * i + u + 1)
            nc.scalar.copy(x_at(x_hi, i, u), x_bank()).then_inc(x_hi_done, 1)

        def out_(i, g):
            need(act, mm_done, 8 * i + g + 1)
            k, half = g % 4 // 2, g % 2
            if g < 4:
                need(act, sil_done, 4 * i + g - 1)
                src = MM[g % 2][:, :].rearrange("p (b t) -> p b t", t=SEQ)
                nc.scalar.activation(x_mid[:, g % 2, :, :], src, ACT.Identity, bias=mid_bias[:, half:half + 1],
                                     scale=vec[:, C_CONV + 3 * half + 1:C_CONV + 3 * half + 2])
                nc.scalar.activation(x_pad[:, g % 2, :, 1:SEQ + 1], src, ACT.Identity,
                                     bias=vec[:, C_W1B + half:C_W1B + half + 1]).then_inc(mm_evac, 1)
            else:
                at = v_sb[:, half, bass.ds(i * GTOK + k * BLK, BLK)]
                nc.scalar.activation(at, MM[g % 2][:, :], ACT.Silu,
                                     bias=vec[:, C_V1B + half:C_V1B + half + 1]).then_inc(mm_evac, 1)

        def silu(i, g):
            need(act, conv_done, 4 * i + g + 1)
            nc.scalar.activation(x_sil[:, g, :, ::-1], x_mid[:, g % 2, :, :], ACT.Silu).then_inc(sil_done, 1)

        act.wait_ge(pad_zero, 1)
        act.wait_ge(half_set, 1)
        nc.scalar.activation(warm_out[:, 0:1], zero[:, :], ACT.Silu)
        run_phase_a(act, {"cat": cat_hi, "emb": h_out, "hn": hn_hi, "x": x_hi_part, "out": out_, "silu": silu})

        def piece_hi(n):
            src, hi, lo, signal, count = PIECES[n]
            act.wait_ge(signal, count)
            nc.scalar.copy(hi, src).then_inc(w_hi_done, 1)

        for q in range(0, NQ, 2):
            act.wait_ge(ssm_done, q + 1)
            nc.scalar.copy(y_at(q), y_bank(q)).then_inc(y_act, 1)
            if q >= 2:
                piece_hi(q // 2 - 1)

        def zc(e, g):
            n = GROUPS * e + g
            if isinstance(e, int) and e == 0:
                act.wait_ge(z_done, 8 + 2 * g + 2)
            need(act, w2_done, n - 1)
            nc.scalar.copy(zc_hi[:, g % 2, :, :], z_cols(e, g)).then_inc(zc_hi_done, 1)

        def turn2_hi(e, par, g):
            need(act, tr2_done, GROUPS * e + g + 1)
            nc.scalar.copy(h2nT_hi[:, par, :, g * P:(g + 1) * P], tr2_bank()).then_inc(h2nT_hi_done, 1)

        def activate(e, n):
            kind, j, bank = PLAN[n]
            need(act, up_done, UNITS * e + n + 1)
            if kind == SHARED:
                nc.scalar.activation(act_out[:, n % 4, :], ps[bank][:, :], ACT.Silu,
                                     bias=vec[:, C_SB1 + j:C_SB1 + j + 1]).then_inc(act_done, 1)
            else:
                x = (e + (RES - 1)) & (RES - 1) if kind == OLD else e
                nc.scalar.activation(act_out[:, n % 4, :], ps[bank][:, :], ACT.Gelu,
                                     bias=vec[:, bass.ds(C_B1 + 2 * x + j, 1)]).then_inc(act_done, 1)

        def hidden_hi(e, n):
            kind, j, bank = PLAN[n]
            if kind == SHARED:
                need(act, gated, 4 * e + j + 1)
            else:
                need(act, act_done, UNITS * e + n + 1)
            nc.scalar.mul(hid_hi[:, n % 4, :], act_out[:, n % 4, :], 0.5 if kind == SHARED else 0.25).then_inc(hid_hi_done, 1)

        def slot(e, par, ahead, before):
            for n in range(UNITS):
                if ahead and 1 <= n <= 4:
                    zc(e + 1, n - 1)
                if ahead and n >= 5:
                    turn2_hi(e + 1, 1 - par, n - 5)
                activate(e, n)
                if n or before:
                    hidden_hi(*((e, n - 1) if n else (e - 1, UNITS - 1)))
            if ahead:
                turn2_hi(e + 1, 1 - par, GROUPS - 1)

        nc.scalar.activation(warm_out[:, 1:2], zero[:, :], ACT.Gelu)
        zc(0, 0)
        zc(0, 1)
        piece_hi(7)
        zc(0, 2)
        piece_hi(8)
        zc(0, 3)
        for g in range(GROUPS):
            turn2_hi(0, 0, g)
        slot(0, 0, True, False)
        with act.Fori(0, 3) as i:
            slot(2 * i + 1, 1, True, True)
            slot(2 * i + 2, 0, True, True)
        slot(RES - 1, 1, False, True)
        hidden_hi(RES - 1, UNITS - 1)

    @block.vector
    def _(dve):
        nc.vector.memset(x_pad[:, :, :, :], 0.0).then_inc(pad_zero, 1)
        nc.vector.memset(k_row[:, :, :, :].rearrange("p n c w -> p (n c w)").bitcast(F32), 0.0).then_inc(row_zero, 1)

        steps = 0

        def link(ins):
            nonlocal steps
            steps += 1
            ins.then_inc(k_step, 1)
            dve.wait_ge(k_step, steps)

        dve.wait_ge(vec_in, 16)
        for half in range(HALVES):
            nc.vector.tensor_tensor(mid_bias[:, half:half + 1], vec[:, C_W1B + half:C_W1B + half + 1],
                                    vec[:, C_CONV + 3 * half + 1:C_CONV + 3 * half + 2], ALU.mult)
        link(nc.vector.tensor_tensor(power[:, :, 0], vec[:, C_B:C_B + 32], vec[:, C_C:C_C + 32], ALU.mult))
        dve.wait_ge(abar_done, 1)

        def double(k):
            n = 1 << k
            by = abar[:, k, :].rearrange("p (s o) -> p s o", o=1).broadcast_to([P, HALVES * STATES, n])
            link(nc.vector.tensor_tensor(power[:, :, n:2 * n], power[:, :, 0:n], by, ALU.mult))
            if k < 6:
                link(nc.vector.tensor_tensor(abar[:, k + 1, :], abar[:, k, :], abar[:, k, :], ALU.mult))

        def wv_split():
            dve.wait_ge(wa_hi, 2)
            nc.vector.tensor_tensor(wv_lo[:, :, :, :].rearrange("p a k n -> p (a k n)"), raw_a[:, KC * D:],
                                    f32(wv_hi[:, :, :, :].rearrange("p a k n -> p (a k n)")), ALU.subtract).then_inc(wa_lo, 1)

        def sum_states(half, t):
            link(nc.vector.tensor_reduce(k_sum[:, half, t:t + HALF],
                                         power[:, half * STATES:(half + 1) * STATES, t:t + HALF].rearrange("p s t -> p t s"),
                                         AX_X, ALU.add))

        def rows_out():
            link(nc.vector.tensor_tensor(k_sum[:, :, 0], k_sum[:, :, 0], vec[:, C_D:C_D + 2], ALU.add))
            row_hi, row_lo = [k_row[:, SEQ - 1:2 * SEQ - 1, :, w].rearrange("p t c -> p c t") for w in range(2)]
            dve.wait_ge(row_zero, 1)
            link(nc.vector.tensor_copy(row_hi, k_sum[:, :, :]))
            link(nc.vector.tensor_tensor(row_lo, k_sum[:, :, :], row_hi, ALU.subtract))
            assert steps == K_STEPS

        for k in range(6):
            double(k)
        dve.wait_ge(wa_hi, 1)
        nc.vector.tensor_tensor(proj_lo[:, :, :].rearrange("p k n -> p (k n)"), raw_a[:, 0:KC * D],
                                f32(proj_hi[:, :, :].rearrange("p k n -> p (k n)")), ALU.subtract).then_inc(wa_lo, 1)
        beside = {0: lambda: double(6), 1: lambda: sum_states(0, 0), 2: lambda: sum_states(0, HALF), 3: wv_split,
                  4: lambda: sum_states(1, 0), 5: lambda: sum_states(1, HALF), 6: rows_out}

        def cat_lo(i, r):
            need(dve, catT_hi_done, RES * i + r + 1)
            nc.vector.tensor_tensor(catT_lo[:, r % 2, :, :].rearrange("p k n -> p (k n)"), CATP[r % 2][:, 0:CAT],
                                    f32(catT_hi[:, r % 2, :, :].rearrange("p k n -> p (k n)")),
                                    ALU.subtract).then_inc(catT_lo_done, 1)

        def bn_stats(src, m, s_stats):
            nc.vector.bn_stats(stat[:, m, :], src).then_inc(s_stats, 1)

        def bn_aggr(n, m, s_stats, s_aggr):
            need(dve, s_stats, n + 1, pad_zero)
            nc.vector.bn_aggr(mv[:, m, :], stat[:, m, :]).then_inc(s_aggr, 1)

        def add_eps(n, m, s_aggr, s_eps):
            need(dve, s_aggr, n + 1)
            nc.vector.tensor_scalar(rstd[:, m:m + 1], mv[:, m, 1:2], EPS, None, ALU.add).then_inc(s_eps, 1)

        def normalize(n, src, dst, m, s_rstd, s_out):
            need(dve, s_rstd, n + 1)
            nc.vector.tensor_scalar(dst, src, mv[:, m, 0:1], rstd[:, m:m + 1], ALU.subtract, ALU.mult).then_inc(s_out, 1)

        def stats(i, r):
            n = RES * i + r
            need(dve, h_done, n + 1, pad_zero)
            bn_stats(h_ring[:, r % 4, :], r % 4, stats_done)

        def aggr(i, r):
            bn_aggr(RES * i + r, r % 4, stats_done, aggr_done)

        def eps(i, r):
            add_eps(RES * i + r, r % 4, aggr_done, eps_done)

        def norm(i, r):
            n = RES * i + r
            normalize(n, h_ring[:, r % 4, :], hn[:, r % 4, :], r % 4, rstd_done, hn_done)
            if isinstance(i, int) and RES * i + r in beside:
                beside[RES * i + r]()

        def hn_lo(i, pair):
            need(dve, hnT_hi_done, 4 * i + pair + 1)
            nc.vector.tensor_tensor(hnT_at(hnT_lo, i, pair), hn_bank(), f32(hnT_at(hnT_hi, i, pair)),
                                    ALU.subtract).then_inc(hnT_lo_done, 1)

        def x_lo_part(i, u):
            need(dve, x_hi_done, 4 * i + u + 1)
            nc.vector.tensor_tensor(x_at(x_lo, i, u), x_bank(), x_at(x_hi, i, u), ALU.subtract).then_inc(x_lo_done, 1)

        def conv_before(i, g):
            c = C_CONV + 3 * (g % 2)
            need(dve, mm_evac, 8 * i + g + 1)
            nc.vector.scalar_tensor_tensor(x_mid[:, g % 2, :, :], x_pad[:, g % 2, :, 0:SEQ], vec[:, c:c + 1],
                                           x_mid[:, g % 2, :, :], ALU.mult, ALU.add).then_inc(conv_left, 1)

        def conv_after(i, g):
            c = C_CONV + 3 * (g % 2)
            need(dve, conv_left, 4 * i + g + 1)
            nc.vector.scalar_tensor_tensor(x_mid[:, g % 2, :, :], x_pad[:, g % 2, :, 2:SEQ + 2], vec[:, c + 2:c + 3],
                                           x_mid[:, g % 2, :, :], ALU.mult, ALU.add).then_inc(conv_done, 1)

        run_phase_a(dve, {"cat": cat_lo, "stats": stats, "norm": norm, "aggr": aggr, "conv_left": conv_before, "eps": eps,
                            "conv_right": conv_after, "hn": hn_lo, "x": x_lo_part})

        def piece_lo(n):
            src, hi, lo, signal, count = PIECES[n]
            dve.wait_ge(w_hi_done, n + 1)
            nc.vector.tensor_tensor(lo, src, f32(hi), ALU.subtract).then_inc(w_lo_done, 1)

        def z_part(u):
            half, k = u // 8, u % 8
            dve.wait_ge(yt_filled, u + 1)
            at = v_sb[:, half, k * BLK:(k + 1) * BLK]
            nc.vector.tensor_tensor(at, yt_bank(u)[:, :], at, ALU.mult).then_inc(z_done, 1)

        for q in range(1, NQ, 2):
            dve.wait_ge(ssm_done, q + 1)
            nc.vector.tensor_copy(y_at(q), y_bank(q)).then_inc(y_dve, 1)
            if q > NQ // 2:
                z_part(q - NQ // 2 - 1)
                if q < NQ - 1:
                    z_part(q - NQ // 2)
            if q >= 3:
                piece_lo(q // 2 - 1)
        z_part(NQ // 2 - 1)

        def mixer_out(e, par, g):
            n = GROUPS * e + g
            need(dve, w2_done, n + 1)
            need(dve, h_biased, e + 1)
            if g == 0:
                need(dve, o_done, GROUPS * (e - 1))
            at = h2_sb[:, par, g, :]
            nc.vector.tensor_tensor(at, ps[6][:, 0:D], h_in[:, par, g, :], ALU.add).then_inc(h2_done, 1)
            need(dve, h2_done, n + 1, pad_zero)
            bn_stats(at, g, stats2_done)
            bn_aggr(n, g, stats2_done, aggr2_done)
            add_eps(n, g, aggr2_done, eps2_done)

        def mixer_norm(e, par, g):
            normalize(GROUPS * e + g, h2_sb[:, par, g, :], h2n[:, g, :], g, rstd2_done, h2n_done)

        def turn2_lo(e, par, g):
            need(dve, h2nT_hi_done, GROUPS * e + g + 1)
            nc.vector.tensor_tensor(h2nT_lo[:, par, :, g * P:(g + 1) * P], tr2_bank(),
                                    f32(h2nT_hi[:, par, :, g * P:(g + 1) * P]), ALU.subtract).then_inc(h2nT_lo_done, 1)

        def gate(e, n):
            kind, j, bank = PLAN[n]
            if kind == SHARED:
                need(dve, act_done, UNITS * e + n + 1)
                nc.vector.scalar_tensor_tensor(act_out[:, n % 4, :], ps[bank + 1][:, :], vec[:, C_SB3 + j:C_SB3 + j + 1],
                                               act_out[:, n % 4, :], ALU.add, ALU.mult).then_inc(gated, 1)

        def hidden_lo(e, n):
            kind, j, bank = PLAN[n]
            need(dve, hid_hi_done, UNITS * e + n + 1)
            nc.vector.scalar_tensor_tensor(hid_lo[:, n % 4, :], act_out[:, n % 4, :], 0.5 if kind == SHARED else 0.25,
                                           f32(hid_hi[:, n % 4, :]), ALU.mult, ALU.subtract).then_inc(hid_lo_done, 1)

        def finish(e, par, times):
            need(dve, l2_done, UNITS * e + UNITS)
            need(dve, h2_biased, GROUPS * e + GROUPS)
            need(dve, stored[par], times)
            for g in range(GROUPS):
                nc.vector.tensor_tensor(o_sb[:, par, g, :], ps[4 + g // 2][:, (g % 2) * D:(g % 2 + 1) * D],
                                        h2_sb[:, par, g, :], ALU.add).then_inc(o_done, 1)

        def slot(e, par, ahead, before, times=0):
            for n in range(UNITS):
                if n == 2 and before:
                    finish(e - 1, 1 - par, times)
                if ahead and 3 <= n <= 6:
                    mixer_norm(e + 1, 1 - par, n - 3)
                if ahead and 2 <= n <= 5:
                    mixer_out(e + 1, 1 - par, n - 2)
                if ahead and n >= 5:
                    turn2_lo(e + 1, 1 - par, n - 5)
                gate(e, n)
                if n or before:
                    hidden_lo(*((e, n - 1) if n else (e - 1, UNITS - 1)))
            if ahead:
                turn2_lo(e + 1, 1 - par, GROUPS - 1)

        for u in range(8, 14):
            z_part(u)
        mixer_out(0, 0, 0)
        z_part(14)
        z_part(15)
        mixer_out(0, 0, 1)
        mixer_norm(0, 0, 0)
        piece_lo(7)
        mixer_out(0, 0, 2)
        mixer_norm(0, 0, 1)
        turn2_lo(0, 0, 0)
        mixer_out(0, 0, 3)
        piece_lo(8)
        mixer_norm(0, 0, 2)
        turn2_lo(0, 0, 1)
        mixer_norm(0, 0, 3)
        turn2_lo(0, 0, 2)
        turn2_lo(0, 0, 3)
        slot(0, 0, True, False)
        slot(1, 1, True, True)
        slot(2, 0, True, True)
        with dve.Fori(0, 2) as i:
            slot(2 * i + 3, 1, True, True, 16 * i + 16)
            slot(2 * i + 4, 0, True, True, 16 * i + 16)
        slot(RES - 1, 1, False, True, 16 * 3)
        hidden_lo(RES - 1, UNITS - 1)
        finish(RES - 1, 1, 16 * 3)

    @block.tensor
    def _(pe):
        def three(out_, hi, lo, rhs_hi, rhs_lo, start, stop, shared_bank=False):
            kw = {"skip_group_check": True} if shared_bank else {}
            nc.tensor.matmul(out_, hi, rhs_hi, start=start, stop=False, **kw)
            nc.tensor.matmul(out_, hi, rhs_lo, start=False, stop=False, **kw)
            return nc.tensor.matmul(out_, lo, rhs_hi, start=False, stop=stop, **kw)

        def cat_turn(i, r):
            need(pe, gathered[r], 16 * (i + 1))
            need(pe, catT_lo_done, RES * i + r - 1)
            for k in range(KC):
                last = nc.tensor.transpose(CATP[r % 2][:, k * P:(k + 1) * P], cat[:, r, k * P:(k + 1) * P], ident[:, :])
            last.then_inc(cat_tr, 1)

        def embed(i, r):
            n = RES * i + r
            need(pe, catT_lo_done, n + 1)
            need(pe, h_done, n - 1)
            if isinstance(i, int) and n == 0:
                pe.wait_ge(wa_lo, 1)
            for k in range(KC):
                last = three(EMBP[r % 2][:, 0:D], catT_hi[:, r % 2, k, :], catT_lo[:, r % 2, k, :],
                             proj_hi[:, k, :], proj_lo[:, k, :], k == 0, k == KC - 1)
            last.then_inc(emb_done, 1)

        def hn_turn(i, pair):
            need(pe, hn_done, RES * i + 2 * pair + 2)
            need(pe, hnT_lo_done, 4 * i + pair)
            for r in range(2):
                for half in range(HALVES):
                    at = (r * HALVES + half) * P
                    last = nc.tensor.transpose(HNP[:, at:at + P], hn[:, (2 * pair + r) % 4, half * P:(half + 1) * P],
                                               ident[:, :])
            last.then_inc(hn_turned, 1)

        def x_turn(i, u):
            need(pe, sil_done, 4 * i + u + 1)
            need(pe, x_lo_done, 4 * i + u)
            for b in range(4):
                last = nc.tensor.transpose(XP[:, b * P:(b + 1) * P], x_sil[:, u, b, :], ident[:, :])
            last.then_inc(x_turned, 1)

        def project(i, g):
            which, k, half = g // 4, g % 4 // 2, g % 2
            need(pe, hnT_lo_done, 4 * i + 4)
            need(pe, mm_evac, 8 * i + g - 1)
            if isinstance(i, int) and i == 0 and g == 0:
                pe.wait_ge(wa_lo, 2)
            for kk in range(HALVES):
                x_parts = [t[:, bass.ds(i & 1, 1), kk, k * BLK:(k + 1) * BLK].rearrange("p o n -> p (o n)")
                           for t in (hnT_hi, hnT_lo)]
                last = three(MM[g % 2][:, :], wv_hi[:, which, kk, half * P:(half + 1) * P],
                             wv_lo[:, which, kk, half * P:(half + 1) * P], *x_parts, kk == 0, kk == HALVES - 1)
            last.then_inc(mm_done, 1)

        pe.wait_ge(ident_step, 2)
        run_phase_a(pe, {"cat": cat_turn, "emb": embed, "hn": hn_turn, "x": x_turn, "mm": project})

        def y_turn(u):
            half, k = u // 8, u % 8
            if k >= 4:
                pe.wait_ge(z_done, u - 3)
            for b in range(4):
                last = nc.tensor.transpose(yt_bank(u)[:, b * P:(b + 1) * P],
                                           y_sb[:, 4 * k + b, half * P:(half + 1) * P], ident[:, :])
            last.then_inc(yt_filled, 1)

        pe.wait_ge(x_lo_done, 16)
        pe.wait_ge(h_done, RES * GROUPS)
        for q in range(NQ):
            loads = q // TRING
            pe.wait_ge(toep_in[q % TRING], 16 * (1 + 2 * loads))
            if q >= 4:
                pe.wait_ge(y_dve if q % 2 else y_act, (q - 4) // 2 + 1)
            for j in range(CH):
                c = q * CH + j
                at = ps[q % 4][:, j * BATCH:(j + 1) * BATCH]
                t_hi, t_lo = toep(q)[:, j // 2, :, j % 2, 0], toep(q)[:, j // 2, :, j % 2, 1]
                nc.tensor.matmul(at, t_hi, x_hi[:, c, :], start=True, stop=False)
                nc.tensor.matmul(at, t_hi, x_lo[:, c, :], start=False, stop=False)
                last = nc.tensor.matmul(at, t_lo, x_hi[:, c, :], start=False, stop=True)
            last.then_inc(ssm_done, 1)
            if q >= NQ // 2:
                if q == NQ // 2:
                    pe.wait_ge(y_act, NQ // 4)
                    pe.wait_ge(y_dve, NQ // 4)
                y_turn(q - NQ // 2)

        def mixer_mm(e, g):
            n = GROUPS * e + g
            need(pe, zc_lo_done, n + 1)
            need(pe, h2_done, n)
            for k in range(HALVES):
                last = three(ps[6][:, 0:D], zc_hi[:, g % 2, k, :], zc_lo[:, g % 2, k, :],
                             w2_hi[:, k, :], w2_lo[:, k, :], k == 0, k == HALVES - 1)
            last.then_inc(w2_done, 1)

        def mixer_turn(e, g):
            n = GROUPS * e + g
            need(pe, h2n_done, n + 1)
            need(pe, h2nT_lo_done, n)
            for half in range(HALVES):
                last = nc.tensor.transpose(ps[7][:, half * P:(half + 1) * P], h2n[:, g, half * P:(half + 1) * P],
                                           ident[:, :])
            last.then_inc(tr2_done, 1)

        def free_banks(e, n):
            acts, gates = {0: (0, None), 1: (None, 0), 2: (0, None), 3: (2, None), 4: (3, 1), 5: (4, 2), 6: (5, None),
                           7: (None, 3)}[n]
            if acts is not None:
                need(pe, act_done, UNITS * e + acts)
            if gates is not None:
                need(pe, gated, 4 * e + gates)

        def hidden(e, par, n):
            kind, j, bank = PLAN[n]
            free_banks(e, n)
            if kind == NEW and j == 0:
                need(pe, ex_done, e)
            for which in range(2 if kind == SHARED else 1):
                for k in range(HALVES):
                    if kind == SHARED:
                        w_hi = sw_hi[:, 2 * which + k, j * P:(j + 1) * P]
                        w_lo = sw_lo[:, 2 * which + k, j * P:(j + 1) * P]
                    else:
                        m = par if kind == NEW else 1 - par
                        at = slice(k * HR + j * P, k * HR + (j + 1) * P)
                        w_hi, w_lo = ex_hi[m][:, 0, at], ex_lo[m][:, 0, at]
                    last = three(ps[bank + which][:, :], w_hi, w_lo, h2nT_hi[:, par, k, :], h2nT_lo[:, par, k, :],
                                 k == 0, k == HALVES - 1)
            last.then_inc(up_done, 1)

        def second(e, par, n):
            kind, j, bank = PLAN[n]
            need(pe, hid_lo_done, UNITS * e + n + 1)
            if n == 0:
                need(pe, o_done, GROUPS * e)
            if kind == SHARED:
                at = slice(j % 2 * D, (j % 2 + 1) * D)
                w_hi, w_lo = sw_hi[:, 4 + j // 2, at], sw_lo[:, 4 + j // 2, at]
            else:
                m = par if kind == NEW else 1 - par
                w_hi, w_lo = ex_hi[m][:, 1, j * D:(j + 1) * D], ex_lo[m][:, 1, j * D:(j + 1) * D]
            for g in range(GROUPS):
                last = three(ps[4 + g // 2][:, (g % 2) * D:(g % 2 + 1) * D], hid_hi[:, n % 4, g * P:(g + 1) * P],
                             hid_lo[:, n % 4, g * P:(g + 1) * P], w_hi, w_lo, n == 0 and g % 2 == 0, n == UNITS - 1,
                             shared_bank=True)
            last.then_inc(l2_done, 1)

        def slot(e, par, ahead, before):
            need(pe, h2nT_lo_done, GROUPS * e + GROUPS)
            for n in range(UNITS):
                hidden(e, par, n)
                if ahead and n >= 4:
                    mixer_turn(e + 1, n - 4)
                if n >= 2:
                    second(e, par, n - 2)
                elif before:
                    second(e - 1, 1 - par, UNITS - 2 + n)
                if ahead and 1 <= n <= 4:
                    mixer_mm(e + 1, n - 1)

        pe.wait_ge(y_act, NQ // 2)
        pe.wait_ge(y_dve, NQ // 2)
        for u in range(8, 16):
            y_turn(u)
        pe.wait_ge(w_lo_done, 1)
        mixer_mm(0, 0)
        mixer_mm(0, 1)
        mixer_turn(0, 0)
        mixer_mm(0, 2)
        mixer_turn(0, 1)
        mixer_mm(0, 3)
        mixer_turn(0, 2)
        mixer_turn(0, 3)
        pe.wait_ge(w_lo_done, len(PIECES))
        slot(0, 0, True, False)
        with pe.Fori(0, 3) as i:
            slot(2 * i + 1, 1, True, True)
            slot(2 * i + 2, 0, True, True)
        slot(RES - 1, 1, False, True)
        second(RES - 1, 1, UNITS - 2)
        second(RES - 1, 1, UNITS - 1)


def kernel(**inputs):
    import numpy as np
    import concourse.bacc as bacc
    from concourse import mybir as mb
    from concourse.bass_utils import run_bass_kernel_spmd as run

    a = {k: np.asarray(v) for k, v in inputs.items()}

    def tiles(w):
        k, n = w.shape
        return np.ascontiguousarray(w.reshape(k // P, P, n).transpose(1, 0, 2).reshape(P, -1))

    def cols(v):
        v = v.reshape(-1, P, v.size // v.shape[0] if v.ndim > 1 else 1)
        return v.transpose(1, 0, 2).reshape(P, -1)

    def pairs(v):
        return v.reshape(P, -1)

    table = np.zeros((VOCAB, CAT), np.float32)
    proj = np.zeros((CAT, D), np.float32)
    row = col = 0
    for t in range(4):
        e, p = a[f"L0_tok_emb{t}"], a[f"L0_tok_proj{t}"]
        table[row:row + e.shape[0], col:col + e.shape[1]] = e
        proj[col:col + e.shape[1]] = p.T
        row, col = row + e.shape[0], col + e.shape[1]
    small = np.concatenate([cols(a["L0_attn_w1_b"]), cols(a["L0_attn_v1_b"]), cols(a["L0_attn_conv_w"].reshape(D, 3)),
                            pairs(a["L0_attn_A"]), pairs(a["L0_attn_B_ssm"]), pairs(a["L0_attn_C_ssm"]),
                            pairs(a["L0_attn_D_ssm"]), cols(a["L0_ffn_sb1"]), cols(a["L0_ffn_sb3"]),
                            cols(a["L0_ffn_b1"].reshape(-1))], axis=1)
    rows = np.concatenate([a["L0_attn_w2_b"], a["L0_ffn_sb2"], a["L0_ffn_b2"].reshape(-1)])
    w_a = np.concatenate([tiles(proj), tiles(a["L0_attn_w1_w"].T), tiles(a["L0_attn_v1_w"].T)], axis=1)
    w_b = np.concatenate([tiles(a["L0_attn_w2_w"].T), tiles(a["L0_ffn_sw1"]), tiles(a["L0_ffn_sw3"]),
                          tiles(a["L0_ffn_sw2"])], axis=1).reshape(P, 7, BLK)
    w_e = np.stack([np.stack([tiles(a["L0_ffn_w1"][e]), tiles(a["L0_ffn_w2"][e])], axis=1) for e in range(RES)])
    arrays = {"ids": a["x"].reshape(-1), "table": table, "small": small, "rows": rows, "w_a": w_a, "w_b": w_b, "w_e": w_e}
    arrays = {k: np.ascontiguousarray(v) for k, v in arrays.items()}

    nc = bacc.Bacc("TRN2", target_bir_lowering=False, num_devices=1)
    args = [nc.dram_tensor(f"{k}_dram", v.shape, mb.dt.from_np(v.dtype), kind="ExternalInput").ap()
            for k, v in arrays.items()]
    scratch = nc.dram_tensor("kernel_rows_dram", (P, 2 * YLEN), F32, kind="Internal").ap()
    h_rows = nc.dram_tensor("h_rows_dram", (RES, P, GROUPS, D), F32, kind="Internal").ap()
    out = nc.dram_tensor("out_dram", (BATCH * SEQ, D), F32, kind="ExternalOutput").ap()
    tower(nc, *args, scratch, h_rows, out)
    r = run(nc, [{f"{k}_dram": v for k, v in arrays.items()}], core_ids=[0])
    return r.results[0]["out_dram"].reshape(BATCH, SEQ, D)
```

```python
from contextlib import ExitStack

import concourse.bass as bass
from concourse import mybir

F32 = mybir.dt.float32
F32R = mybir.dt.float32r
F16 = mybir.dt.float16
I32 = mybir.dt.int32
ALU = mybir.AluOpType
ACT = mybir.ActivationFunctionType
AX_X = mybir.AxisListType.X

P = 128
BATCH, SEQ, D = 32, 128, 256
VOCAB = 32000
CAT = 384
KC = CAT // P
HALVES = D // P
RES = 8
GROUPS = BATCH * SEQ // (P * RES)
GTOK = P * RES
BLK = 512
STATES = 16
HR = 256
UNITS = 8
EMB_SCALE = float(D) ** 0.5
EPS = 1e-5
CH = 16
NQ = D // CH
TRIGHT, TLEFT = 4, 6
TRING = TRIGHT + TLEFT
YLEN = 256
PAIRS = CH // 2
HALF = SEQ // 2

C_W1B, C_V1B, C_CONV = 0, 2, 4
C_A, C_B, C_C, C_D = 10, 42, 74, 106
C_SB1, C_SB3, C_B1 = 108, 112, 116
NSMALL = 132

OLD, SHARED, NEW = range(3)
PLAN = [(OLD, 0, 0), (OLD, 1, 1), (SHARED, 0, 2), (SHARED, 1, 0), (SHARED, 2, 2), (SHARED, 3, 0), (NEW, 0, 2),
        (NEW, 1, 3)]

LEAD = 5
X1, V = range(2)
PROJ = [(X1, 0), (X1, 1), (V, 0), (X1, 2), (V, 1), (X1, 3), (V, 2), (V, 3)]
X1_AT = [PROJ.index((X1, g)) for g in range(4)]


def slot_of(r):
    return 3 * r % RES


def tower(nc, ids, table, small, rows, w_a, w_b, w_e, kernel_rows, h_rows, out):
    ctx = ExitStack()
    with ctx:
        _tower(nc, ctx, ids, table, small, rows, w_a, w_b, w_e, kernel_rows, h_rows, out)


def _tower(nc, ctx, ids, table, small, rows, w_a, w_b, w_e, kernel_rows, h_rows, out):
    def sem(name):
        return ctx.enter_context(nc.semaphore(name))

    def sb(stack, name, shape, dt, side):
        return stack.enter_context(nc.sbuf_tensor(name, shape, dt, side=side))

    R, L = "right", "left"
    v_sb = sb(ctx, "v_sb", [P, HALVES, BATCH * SEQ], F32, R)
    w2_hi = sb(ctx, "w2_hi", [P, HALVES, D], F32R, R)
    w2_lo = sb(ctx, "w2_lo", [P, HALVES, D], F32R, R)
    bias_e = sb(ctx, "bias_e", [P, RES, D], F32, R)
    bias_row = sb(ctx, "bias_row", [P, 2, D], F32, R)
    w2_bias = bias_row[:, 0:1, :]
    vec = sb(ctx, "vec", [P, NSMALL], F32, R)
    ident = sb(ctx, "ident", [P, P], F32, R)
    stat = sb(ctx, "stat", [P, 4, 6], F32, R)
    mv = sb(ctx, "mv", [P, 4, 2], F32, R)
    rstd = sb(ctx, "rstd", [P, 4], F32, R)
    shift = sb(ctx, "shift", [P, 4], F32, R)
    minus_half = sb(ctx, "minus_half", [P, 1], F32, R)
    zero = sb(ctx, "zero", [P, 1], F32, R)
    warm_out = sb(ctx, "warm_out", [P, 2], F32, R)
    mid_bias = sb(ctx, "mid_bias", [P, HALVES], F32, R)

    ssm_mem = ExitStack()
    x_sb = sb(ssm_mem, "x_sb", [P, D, 2, BATCH], F16, R)
    x_hi, x_lo = x_sb[:, :, 0, :], x_sb[:, :, 1, :]
    toep_r = sb(ssm_mem, "toep_r", [P, TRIGHT, PAIRS, SEQ, 2, 2], F16, R)
    flat = toep_r[:, :, :, :, :, :].rearrange("p a j t c w -> p (a j t c w)").bitcast(F32)
    power = flat[:, 0:HALVES * STATES * SEQ].rearrange("p (s t) -> p s t", t=SEQ)
    raw_at = HALVES * STATES * SEQ
    raw_a = flat[:, raw_at:raw_at + (KC + 4) * D]
    k_sum = flat[:, raw_at + (KC + 4) * D:raw_at + (KC + 5) * D].rearrange("p (h t) -> p h t", t=SEQ)

    mem_a = ExitStack()
    x_ids = sb(mem_a, "x_ids", [P, GROUPS, RES], I32, L)
    idx = sb(mem_a, "idx", [P, RES], I32, L)
    cat = sb(mem_a, "cat", [P, RES, CAT], F32, L)
    catT_hi = sb(mem_a, "catT_hi", [P, 2, KC, P], F32R, L)
    catT_lo = sb(mem_a, "catT_lo", [P, 2, KC, P], F32R, L)
    hn = sb(mem_a, "hn", [P, 4, D], F32, L)
    proj_hi = sb(mem_a, "proj_hi", [P, KC, D], F32R, L)
    proj_lo = sb(mem_a, "proj_lo", [P, KC, D], F32R, L)
    h_ring = sb(mem_a, "h_ring", [P, 4, D], F32, L)
    hnT = sb(mem_a, "hnT", [P, 2, 2, HALVES, GTOK], F32R, L)
    hnT_hi, hnT_lo = hnT[:, :, 0, :, :], hnT[:, :, 1, :, :]
    x_pad = sb(mem_a, "x_pad", [P, 2, 4, SEQ + 2], F32, L)
    x_mid = sb(mem_a, "x_mid", [P, 2, 4, SEQ], F32, L)
    x_sil = sb(mem_a, "x_sil", [P, 4, 4, SEQ], F32, L)
    wv_hi = sb(mem_a, "wv_hi", [P, 2, HALVES, D], F32R, L)
    wv_lo = sb(mem_a, "wv_lo", [P, 2, HALVES, D], F32R, L)
    abar = sb(mem_a, "abar", [P, 7, HALVES * STATES], F32, L)
    k_row = sb(mem_a, "k_row", [P, YLEN, 2, 2], F16, L)
    mem_a.close()

    mem_t = ExitStack()
    toep_l = sb(mem_t, "toep_l", [P, TLEFT, PAIRS, SEQ, 2, 2], F16, L)
    mem_t.close()
    zc_hi = sb(ctx, "zc_hi", [P, GROUPS, HALVES, P], F32R, L)
    zc_lo = sb(ctx, "zc_lo", [P, GROUPS, HALVES, P], F32R, L)
    ex1_hi = sb(ctx, "ex1_hi", [P, 2, BLK], F32R, L)
    ex1_lo = sb(ctx, "ex1_lo", [P, 2, BLK], F32R, L)
    h_in = sb(ctx, "h_in", [P, 2, GROUPS, D], F32, L)
    sw_hi = sb(ctx, "sw_hi", [P, 6, BLK], F32R, L)
    sw_lo = sb(ctx, "sw_lo", [P, 6, BLK], F32R, L)
    ex0_hi = sb(ctx, "ex0_hi", [P, 2, BLK], F32R, L)
    ex0_lo = sb(ctx, "ex0_lo", [P, 2, BLK], F32R, L)
    stage = sb(ctx, "stage", [P, 4, BLK], F32, L)
    mem_y = ExitStack()
    y_sb = sb(mem_y, "y_sb", [P, BATCH, D], F32, L)
    mem_y.close()
    ssm_mem.close()

    h2_sb = sb(ctx, "h2_sb", [P, 2, GROUPS, D], F32, R)
    h2n = sb(ctx, "h2n", [P, 4, D], F32, R)
    h2nT_hi = sb(ctx, "h2nT_hi", [P, 2, HALVES, BLK], F32R, R)
    h2nT_lo = sb(ctx, "h2nT_lo", [P, 2, HALVES, BLK], F32R, R)
    hid_hi = sb(ctx, "hid_hi", [P, 4, BLK], F32R, R)
    hid_lo = sb(ctx, "hid_lo", [P, 4, BLK], F32R, R)
    act_out = sb(ctx, "act_out", [P, 4, BLK], F32, R)
    o_sb = sb(ctx, "o_sb", [P, 2, GROUPS, D], F32, R)
    ex_hi, ex_lo = [ex0_hi, ex1_hi], [ex0_lo, ex1_lo]

    ps = [ctx.enter_context(nc.psum_tensor(f"ps{i}", [P, BLK], F32)) for i in range(8)]
    CATP, EMBP, HNP, XP, MM = ps[0:2], ps[2:4], ps[4], ps[5], ps[6:8]

    ids_in = sem("ids_in")
    vec_in = sem("vec_in")
    wa_in = sem("wa_in")
    rows_in = sem("rows_in")
    ident_step = sem("ident_step")
    half_set = sem("half_set")
    pad_zero = sem("pad_zero")
    row_zero = sem("row_zero")
    wa_hi = sem("wa_hi")
    wa_lo = sem("wa_lo")
    wv_lo_done = sem("wv_lo_done")
    abar_done = sem("abar_done")
    k_step = sem("k_step")
    k_out = sem("k_out")
    bias_step = sem("bias_step")
    idx_copied = sem("idx_copied")
    cat_zero = sem("cat_zero")
    gathered = [sem(f"gathered{r}") for r in range(RES)]
    cat_tr = sem("cat_tr")
    catT_hi_done = sem("catT_hi_done")
    catT_lo_done = sem("catT_lo_done")
    emb_done = sem("emb_done")
    h_done = sem("h_done")
    h_stored = [sem(f"h_stored{s}") for s in range(4)]
    stats_done = sem("stats_done")
    aggr_done = sem("aggr_done")
    eps_done = sem("eps_done")
    rstd_done = sem("rstd_done")
    shift_done = sem("shift_done")
    hn_first = sem("hn_first")
    hn_done = sem("hn_done")
    hn_turned = sem("hn_turned")
    hnT_hi_done = sem("hnT_hi_done")
    hnT_lo_done = sem("hnT_lo_done")
    mm_done = sem("mm_done")
    mm_evac = sem("mm_evac")
    conv_left = sem("conv_left")
    conv_done = sem("conv_done")
    sil_done = sem("sil_done")
    x_turned = sem("x_turned")
    x_hi_done = sem("x_hi_done")
    x_lo_done = sem("x_lo_done")
    toep_in = [sem(f"toep_in{s}") for s in range(TRING)]
    ssm_done = sem("ssm_done")
    y_low = sem("y_low")
    y_done = sem("y_done")
    yt_filled = sem("yt_filled")
    z_done = sem("z_done")
    piece_loaded = [sem(f"piece_in{n}") for n in range(9)]
    w_hi_done = sem("w_hi_done")
    w_lo_done = [sem("w_lo_dve"), sem("w_lo_pool")]
    ex_in = [sem(f"ex_in{s}") for s in range(2)]
    ex_hi_done = sem("ex_hi_done")
    ex_done = sem("ex_done")
    h_back = [sem(f"h_back{s}") for s in range(2)]
    h_biased = sem("h_biased")
    zc_hi_done = sem("zc_hi_done")
    zc_lo_done = sem("zc_lo_done")
    w2_done = sem("w2_done")
    h2_done = sem("h2_done")
    stats2_done = sem("stats2_done")
    aggr2_done = sem("aggr2_done")
    eps2_done = sem("eps2_done")
    rstd2_done = sem("rstd2_done")
    h2n_done = sem("h2n_done")
    h2_biased = sem("h2_biased")
    tr2_done = sem("tr2_done")
    h2nT_hi_done = sem("h2nT_hi_done")
    h2nT_lo_done = sem("h2nT_lo_done")
    up_done = sem("up_done")
    act_done = sem("act_done")
    gated = sem("gated")
    hid_hi_done = sem("hid_hi_done")
    hid_lo_done = sem("hid_lo_done")
    l2_done = sem("l2_done")
    l2_half_done = sem("l2_half_done")
    o_done = sem("o_done")
    stored = [sem(f"stored{s}") for s in range(2)]

    def f32(ap):
        return ap.bitcast(F32)

    def need(eng, signal, count, passed=None, value=1):
        if isinstance(count, int):
            if count > 0:
                eng.wait_ge(signal, count)
            return
        if passed is not None:
            eng.compute_val(count)
            eng.wait_ge(passed, value)
        eng.wait_ge(signal, count)

    def phase_a(i):
        def there(back):
            return 0 <= i - back < GROUPS if isinstance(i, int) else True
        out_ = []

        def add(name, back, index):
            if there(back):
                out_.append((name, i - back if back else i, index))

        def behind(name, r, lag, positions=range(RES)):
            at = (r - 3 - lag) % RES
            if at in positions:
                add(name, 1 if r >= 3 + lag else 2, positions.index(at))

        for r in range(RES):
            add("cat", 0, r)
            behind("out", r, 1)
            add("emb", 0, r - 1) if r else add("emb", 1, RES - 1)
            add("stats", 0, r - 1) if r else add("stats", 1, RES - 1)
            add("norm", 0, r - 2) if r >= 2 else add("norm", 1, RES - 2 + r)
            add("aggr", 0, r - 1) if r else add("aggr", 1, RES - 1)
            behind("conv_left", r, 1, X1_AT)
            add("eps", 0, r - 1) if r else add("eps", 1, RES - 1)
            behind("conv_right", r, 1, X1_AT)
            if r in (0, 2):
                add("hn", 1, 2 + r // 2)
            if r in (4, 6):
                add("hn", 0, (r - 4) // 2)
            behind("x", r, 3, X1_AT)
            behind("silu", r, 2, X1_AT)
            add("mm", 2, 5 + r) if r < 3 else add("mm", 1, r - 3)
        return out_

    def need_hn(eng, i, r):
        if isinstance(i, int) and i <= 0:
            if i == 0:
                eng.wait_ge(hn_first, r + 1)
        else:
            need(eng, hn_done, RES * (i - 1) + r + 1)

    def run_phase_a(eng, tasks):
        def body(i):
            for name, group, index in phase_a(i):
                if name in tasks:
                    tasks[name](group, index)

        body(0)
        body(1)
        with eng.Fori(2, GROUPS) as i:
            body(i)
        body(GROUPS)
        body(GROUPS + 1)

    K_STEPS = 1 + 8 + 6 + 4 + 3
    BIAS_STEPS = 3 + 2 * RES

    def hn_bank():
        return HNP[:, :].rearrange("c (r h p) -> c h p r", r=2, h=HALVES)

    def hnT_at(t, i, pair):
        v = t[:, bass.ds(i & 1, 1), :, :].rearrange("c o h (p r) -> c (o h) p r", r=RES)
        return v[:, :, :, 2 * pair:2 * pair + 2]

    def x_bank():
        return XP[:, :].rearrange("u (b c) -> u b c", b=4)

    def x_at(t, i, u):
        k, half = u // 2, u % 2
        v = t[:, half * P:(half + 1) * P, :].rearrange("u c b -> u b c")
        return v[:, bass.ds(8 * i + 4 * k, 4), :]

    def toep(q):
        slot = q % TRING
        return toep_r[:, slot, :, :, :, :] if slot < TRIGHT else toep_l[:, slot - TRIGHT, :, :, :, :]

    def y_part(q, bank, w):
        v = ps[2 * (q % 2) + bank][:, :].rearrange("t (c w b) -> t c w b", w=2, b=BATCH)
        return v[:, :, w, :]

    def y_at(q, bank):
        first = q * CH + bank * CH // 2
        return y_sb[:, :, first:first + CH // 2].rearrange("t b c -> t c b")

    def yt_bank(u):
        return ps[4 * (1 - u // 8) + u % 4]

    def tr2_bank(e, g):
        bank = ps[5 if isinstance(e, int) and e == 0 and g % 2 else 7]
        return bank[:, 0:D].rearrange("c (h p) -> c h p", h=HALVES)

    def w2_bank(e, g):
        return ps[(4, 5, 6, 4)[g] if isinstance(e, int) and e == 0 else 6]

    def z_cols(e, g):
        r = (3 * e) & (RES - 1)
        v = v_sb[:, :, g * GTOK:(g + 1) * GTOK].rearrange("c h (p r) -> c h r p", r=RES)
        return v[:, :, bass.ds(r, 1), :].rearrange("c h o p -> c h (o p)")

    spare = o_sb[:, :, :, :].rearrange("p a g c -> p (a g c)")
    raws = [stage[:, 0, :], stage[:, 2:4, :], stage[:, 1, :]] + [spare[:, n * BLK:(n + 1) * BLK] for n in range(4)]
    raws += [stage[:, 0, :], stage[:, 2:4, :]]
    his = [w2_hi[:, :, :].rearrange("p k n -> p (k n)"), ex1_hi[:, :, :]] + [sw_hi[:, n, :] for n in range(6)]
    los = [w2_lo[:, :, :].rearrange("p k n -> p (k n)"), ex1_lo[:, :, :]] + [sw_lo[:, n, :] for n in range(6)]
    his, los = his + [ex0_hi[:, :, :]], los + [ex0_lo[:, :, :]]
    sources = [w_b[:, 0, :], w_e[RES - 1]] + [w_b[:, n, :] for n in range(1, 7)] + [w_e[0]]
    LO_BY = (0, 1, 0, 0, 0, 0, 0, 0, 1)

    def need_piece(eng, n):
        eng.wait_ge(w_lo_done[LO_BY[n]], LO_BY[:n + 1].count(LO_BY[n]))

    block = ctx.enter_context(nc.Block())

    @block.sync
    def _(sp):
        sp.dma_start(x_ids[:, :, :], ids.rearrange("(g p r) -> p g r", p=P, r=RES)).then_inc(ids_in, 16)
        sp.dma_start(vec[:, :], small).then_inc(vec_in, 16)
        sp.dma_start(raw_a[:, 0:KC * D], w_a[:, 0:KC * D]).then_inc(wa_in, 16)

        def h_store(i, r):
            need(sp, h_done, RES * i + r + 1, ids_in, 16)
            sp.dma_start(h_rows[slot_of(r), :, bass.ds(i, 1), :].rearrange("p o c -> p (o c)"),
                         h_ring[:, r % 4, :]).then_inc(h_stored[r % 4], 16)

        def h_load(e, par):
            sp.dma_start(h_in[:, par, :, :],
                         h_rows[bass.ds(e, 1), :, :, :].rearrange("o p g c -> (o p) g c")).then_inc(h_back[par], 16)

        def toep_part(q, first, n, t):
            src = bass.AP(kernel_rows.tensor, q * PAIRS * 2 * YLEN + 2 * (first + t),
                          [[2, n], [2 * YLEN, PAIRS], [1, 2 * (SEQ - t)]])
            dst = toep(q)[first:first + n, :, t:, :, :].rearrange("p j t c w -> p j (t c w)").bitcast(F32)
            sp.dma_start(dst, src).then_inc(toep_in[q % TRING], 16)

        def toep_load(q):
            if q < TRING:
                toep_part(q, 0, P, 0)
            else:
                toep_part(q, 0, HALF, HALF)
                toep_part(q, HALF, HALF, 0)

        for r in range(RES):
            h_store(0, r)
            if r == 0:
                sp.dma_start(raw_a[:, KC * D:], w_a[:, KC * D:]).then_inc(wa_in, 16)
        sp.dma_start(bias_row[:, 0:1, :], bass.AP(rows.tensor, D, [[0, P], [D, 1], [1, D]])).then_inc(rows_in, 16)
        sp.dma_start(bias_e[:, :, :], bass.AP(rows.tensor, 2 * D, [[0, P], [D, RES], [1, D]])).then_inc(rows_in, 16)
        for r in range(RES):
            h_store(1, r)
            if r == 1:
                sp.wait_ge(k_step, K_STEPS)
                sp.dma_start(kernel_rows, k_row[:, :, :, :].rearrange("p n c w -> p (n c w)").bitcast(F32)
                             ).then_inc(k_out, 16)
                sp.wait_ge(k_out, 16)
                sp.wait_ge(wv_lo_done, 2)
            if r >= RES - TRIGHT:
                toep_load(r - RES + TRIGHT)
        with sp.Fori(2, GROUPS) as i:
            for r in range(RES):
                h_store(i, r)
        sp.wait_ge(hn_turned, 4 * GROUPS)
        sp.wait_ge(catT_lo_done, RES * GROUPS)
        for s in range(4):
            sp.wait_ge(h_stored[s], 16 * 2 * GROUPS)
        for q in range(TRIGHT, NQ):
            if q == TRIGHT + 4:
                sp.wait_ge(mm_done, 8 * (GROUPS - 1))
            if q >= TRING:
                sp.wait_ge(ssm_done, 2 * (q - TRING + 1))
            toep_load(q)

        def store(e, par):
            need(sp, o_done, GROUPS * e + GROUPS, ids_in, 16)
            r = (3 * e) & (RES - 1)
            dst = out.rearrange("(g p r) c -> r p g c", p=P, r=RES)
            sp.dma_start(dst[bass.ds(r, 1), :, :, :].rearrange("o p g c -> (o p) g c"),
                         o_sb[:, par, :, :]).then_inc(stored[par], 16)

        def piece_in(n):
            sp.dma_start(raws[n], sources[n]).then_inc(piece_loaded[n], 16)

        sp.wait_ge(ssm_done, 2 * (TRING - 3))
        h_load(0, 0)
        sp.wait_ge(bias_step, BIAS_STEPS)
        sp.dma_start(w2_bias, bass.AP(rows.tensor, 0, [[0, P], [D, 1], [1, D]])).then_inc(rows_in, 16)
        piece_in(0)
        piece_in(1)
        h_load(1, 1)
        piece_in(2)
        sp.wait_ge(ssm_done, 2 * NQ)
        for n in range(3, 7):
            piece_in(n)
        need_piece(sp, 0)
        piece_in(7)
        need_piece(sp, 1)
        piece_in(8)
        sp.wait_ge(h2_done, GROUPS)
        h_load(2, 0)
        store(0, 0)
        h_load(3, 1)
        with sp.Fori(0, 2) as i:
            store(2 * i + 1, 1)
            h_load(2 * i + 4, 0)
            store(2 * i + 2, 0)
            h_load(2 * i + 5, 1)
        store(RES - 3, 1)
        store(RES - 2, 0)
        dst = out.rearrange("(g p r) c -> r p g c", p=P, r=RES)[3 * (RES - 1) % RES]
        for g in range(GROUPS):
            sp.wait_ge(o_done, GROUPS * (RES - 1) + g + 1)
            sp.dma_start(dst[:, g, :], o_sb[:, 1, g, :]).then_inc(stored[1], 16)
        sp.wait_ge(stored[0], 16 * RES // 2)
        sp.wait_ge(stored[1], 16 * (RES // 2 - 1 + GROUPS))

    @block.gpsimd
    def _(pool):
        nc.gpsimd.memset(ident[:, :], 0.0).then_inc(ident_step, 1)
        nc.gpsimd.memset(zero[:, :], 0.0)
        nc.gpsimd.memset(minus_half[:, :], -0.5).then_inc(half_set, 1)

        def gather(i, r):
            n = RES * i + r + 1
            if not isinstance(i, int) or i:
                need(pool, catT_lo_done, n - RES, half_set)
            nc.gpsimd.memset(cat[:, r, :], 0.0).then_inc(cat_zero, 1)
            if isinstance(i, int) and i == 0 and r == 0:
                pool.wait_ge(ids_in, 16)
            nc.gpsimd.tensor_copy(idx[:, r:r + 1], x_ids[:, bass.ds(i, 1), r:r + 1].rearrange("p o r -> p (o r)")
                                  ).then_inc(idx_copied, 1)
            need(pool, idx_copied, n, half_set)
            need(pool, cat_zero, n, half_set)
            pool.indirect_dma_start(cat[:, r, :], None, table,
                                    bass.IndirectOffsetOnAxis(ap=idx[:, r:r + 1], axis=0),
                                    bounds_check=VOCAB - 1, oob_is_err=False).then_inc(gathered[r], 16)

        def power_step(n, m, s_eps, s_rstd):
            need(pool, s_eps, n + 1, half_set)
            nc.gpsimd.tensor_tensor(rstd[:, m:m + 1], rstd[:, m:m + 1], minus_half[:, :], ALU.pow).then_inc(s_rstd, 1)

        def group(i):
            for r in range(RES):
                if r or not isinstance(i, int) or i:
                    power_step(RES * i + r - 1, (r - 1) % 4, eps_done, rstd_done)
                if r + LEAD < RES:
                    gather(i, r + LEAD)
                elif not isinstance(i, int) or i + 1 < GROUPS:
                    gather(i + 1, r + LEAD - RES)
                if isinstance(i, int) and i == 0 and r in (4, 6):
                    m = (r - 4) // 2
                    pool.wait_ge(wa_hi, 2)
                    nc.gpsimd.tensor_tensor(wv_lo[:, m, :, :].rearrange("p k n -> p (k n)"),
                                            raw_a[:, (KC + 2 * m) * D:(KC + 2 * m + 2) * D],
                                            f32(wv_hi[:, m, :, :].rearrange("p k n -> p (k n)")),
                                            ALU.subtract).then_inc(wv_lo_done, 1)

        gather(0, 0)
        pool.wait_ge(ident_step, 1)
        nc.gpsimd.affine_select(out=ident[:, :], in_=ident[:, :], compare_op=ALU.not_equal, fill=1.0, base=0,
                                pattern=[[-1, P]], channel_multiplier=1).then_inc(ident_step, 1)
        for r in range(1, LEAD):
            gather(0, r)
        group(0)
        with pool.Fori(1, GROUPS - 1) as i:
            group(i)
        group(GROUPS - 1)
        power_step(RES * GROUPS - 1, (RES - 1) % 4, eps_done, rstd_done)

        steps = 0

        def link(ins):
            nonlocal steps
            steps += 1
            ins.then_inc(bias_step, 1)
            pool.wait_ge(bias_step, steps)

        pool.wait_ge(rows_in, 32)
        link(nc.gpsimd.tensor_scalar(bias_e[:, :, :], bias_e[:, :, :], 0.25, None, ALU.mult))
        link(nc.gpsimd.tensor_scalar(bias_row[:, 0, :], bias_row[:, 0, :], 0.5, None, ALU.mult))
        link(nc.gpsimd.tensor_copy(bias_row[:, 1, :], bias_e[:, RES - 1, :]))
        for e in range(RES - 1, -1, -1):
            before = bias_e[:, e - 1, :] if e else bias_row[:, 1, :]
            link(nc.gpsimd.tensor_tensor(bias_e[:, e, :], bias_e[:, e, :], before, ALU.add))
            link(nc.gpsimd.tensor_tensor(bias_e[:, e, :], bias_e[:, e, :], bias_row[:, 0, :], ALU.add))
        assert steps == BIAS_STEPS

        def expert_in(n, par):
            x = (n + (RES - 1)) & (RES - 1)
            pool.dma_start(stage[:, 2 * par:2 * par + 2, :],
                           w_e[bass.ds(x, 1), :, :, :].rearrange("o p k n -> (o p) k n")).then_inc(ex_in[par], 16)

        def expert_split(n, par, times):
            to = 1 - par
            need(pool, ex_in[par], 16 * times - 16, half_set)
            nc.gpsimd.tensor_copy(ex_hi[to][:, :, :], stage[:, 2 * par:2 * par + 2, :]).then_inc(ex_hi_done, 1)
            need(pool, ex_hi_done, n - 1, half_set)
            nc.gpsimd.tensor_tensor(ex_lo[to][:, :, :], stage[:, 2 * par:2 * par + 2, :], f32(ex_hi[to][:, :, :]),
                                    ALU.subtract).then_inc(ex_done, 1)
            need(pool, ex_done, n - 1, half_set)

        def mixer_lo(e, g):
            need(pool, zc_hi_done, GROUPS * e + g + 1, half_set)
            nc.gpsimd.tensor_tensor(zc_lo[:, g, :, :], z_cols(e, g), f32(zc_hi[:, g, :, :]),
                                    ALU.subtract).then_inc(zc_lo_done, 1)

        def mixer_bias(e, par, g):
            need(pool, h2n_done, GROUPS * e + g + 1, half_set)
            at = h2_sb[:, par, g, :]
            nc.gpsimd.tensor_tensor(at, at, bias_e[:, bass.ds(e, 1), :].rearrange("p o c -> p (o c)"),
                                    ALU.add).then_inc(h2_biased, 1)

        def mixer_1():
            for g in range(2):
                mixer_lo(1, g)
                mixer_bias(0, 0, g)
            for g in range(GROUPS):
                power_step(GROUPS + g, g, eps2_done, rstd2_done)
                if g < 2:
                    mixer_bias(0, 0, g + 2)
                    mixer_lo(1, g + 2)
            add_w2_bias(0, 2)
            for g in range(GROUPS):
                mixer_bias(1, 1, g)

        def mixer(e, par, times):
            mixer_lo(e, 0)
            mixer_lo(e, 1)
            for g in range(GROUPS):
                power_step(GROUPS * e + g, g, eps2_done, rstd2_done)
                if g == GROUPS - 1 and times is not None:
                    add_w2_bias(1 - par, times)
                mixer_bias(e, par, g)
                if g + 2 < GROUPS:
                    mixer_lo(e, g + 2)

        def add_w2_bias(par, times):
            need(pool, h_back[par], 16 * times, half_set)
            at = h_in[:, par, :, :]
            nc.gpsimd.tensor_tensor(at, at, w2_bias[:, :, :].broadcast_to([P, GROUPS, D]), ALU.add).then_inc(h_biased, 1)

        def slot(e, par, times, load=True, bias=True):
            if isinstance(e, int) and e == 0:
                mixer_1()
            else:
                mixer(e + 1, 1 - par, times if bias else None)
            if load:
                expert_in(e + 3, 1 - par)
            need(pool, l2_done, UNITS * e + 2, half_set)
            expert_split(e + 2, par, times)

        def piece_lo(n):
            pool.wait_ge(w_hi_done, n + 1)
            nc.gpsimd.tensor_tensor(los[n], raws[n], f32(his[n]), ALU.subtract).then_inc(w_lo_done[1], 1)

        pool.wait_ge(rows_in, 48)
        add_w2_bias(0, 1)
        piece_lo(1)
        for g in range(GROUPS):
            mixer_lo(0, g)
        for g in range(GROUPS):
            power_step(g, g, eps2_done, rstd2_done)
        add_w2_bias(1, 1)
        piece_lo(8)
        pool.wait_ge(w_lo_done[0], LO_BY.count(0))
        expert_in(2, 0)
        slot(0, 0, 2)
        with pool.Fori(0, 2) as i:
            slot(2 * i + 1, 1, i + 2)
            slot(2 * i + 2, 0, i + 3)
        slot(5, 1, 4)
        slot(6, 0, 5, load=False, bias=False)

    @block.scalar
    def _(act):
        act.wait_ge(vec_in, 16)
        nc.scalar.activation(abar[:, 0, :], vec[:, C_A:C_A + 32], ACT.Sigmoid).then_inc(abar_done, 1)
        act.wait_ge(half_set, 1)
        nc.scalar.activation(warm_out[:, 0:1], zero[:, :], ACT.Silu)
        act.wait_ge(wa_in, 16)
        nc.scalar.copy(proj_hi[:, :, :].rearrange("p k n -> p (k n)"), raw_a[:, 0:KC * D]).then_inc(wa_hi, 1)

        def cat_hi(i, r):
            n = RES * i + r
            need(act, cat_tr, n + 1)
            nc.scalar.copy(catT_hi[:, r % 2, :, :].rearrange("p k n -> p (k n)"), CATP[r % 2][:, 0:CAT]
                           ).then_inc(catT_hi_done, 1)

        def h_out(i, r):
            n = RES * i + r
            need(act, emb_done, n + 1)
            uses = 2 * i + r // 4
            need(act, h_stored[r % 4], 16 * uses)
            need_hn(act, i - 1 if r < 4 else i, (r - 4) % RES)
            nc.scalar.mul(h_ring[:, r % 4, :], EMBP[r % 2][:, 0:D], EMB_SCALE).then_inc(h_done, 1)

        def norm(i, r):
            if not isinstance(i, int) or i:
                return
            act.wait_ge(shift_done, r + 1)
            need(act, hn_turned, r // 2 - 1)
            nc.scalar.activation(hn[:, r % 4, :], h_ring[:, r % 4, :], ACT.Identity, bias=shift[:, r % 4:r % 4 + 1],
                                 scale=rstd[:, r % 4:r % 4 + 1]).then_inc(hn_first, 1)
            if r == 1:
                act.wait_ge(wa_in, 32)
                nc.scalar.copy(wv_hi[:, :, :, :].rearrange("p a k n -> p (a k n)"), raw_a[:, KC * D:]).then_inc(wa_hi, 1)

        def hn_hi(i, pair):
            need(act, hn_turned, 4 * i + pair + 1)
            nc.scalar.copy(hnT_at(hnT_hi, i, pair), hn_bank()).then_inc(hnT_hi_done, 1)

        def x_hi_part(i, u):
            need(act, x_turned, 4 * i + u + 1)
            nc.scalar.copy(x_at(x_hi, i, u), x_bank()).then_inc(x_hi_done, 1)

        def out_(i, at):
            kind, g = PROJ[at]
            need(act, mm_done, 8 * i + at + 1)
            k, half = g // 2, g % 2
            if kind == X1:
                need(act, sil_done, 4 * i + g - 1)
                src = MM[at % 2][:, :].rearrange("p (b t) -> p b t", t=SEQ)
                nc.scalar.activation(x_mid[:, g % 2, :, :], src, ACT.Identity, bias=mid_bias[:, half:half + 1],
                                     scale=vec[:, C_CONV + 3 * half + 1:C_CONV + 3 * half + 2])
                nc.scalar.activation(x_pad[:, g % 2, :, 1:SEQ + 1], src, ACT.Identity,
                                     bias=vec[:, C_W1B + half:C_W1B + half + 1]).then_inc(mm_evac, 1)
            else:
                dst = v_sb[:, half, bass.ds(i * GTOK + k * BLK, BLK)]
                nc.scalar.activation(dst, MM[at % 2][:, :], ACT.Silu,
                                     bias=vec[:, C_V1B + half:C_V1B + half + 1]).then_inc(mm_evac, 1)

        def silu(i, g):
            need(act, conv_done, 4 * i + g + 1)
            nc.scalar.activation(x_sil[:, g, :, ::-1], x_mid[:, g % 2, :, :], ACT.Silu).then_inc(sil_done, 1)

        act.wait_ge(pad_zero, 1)
        run_phase_a(act, {"cat": cat_hi, "out": out_, "emb": h_out, "norm": norm, "hn": hn_hi, "x": x_hi_part,
                            "silu": silu})

        def piece_hi(n):
            act.wait_ge(piece_loaded[n], 16)
            nc.scalar.copy(his[n], raws[n]).then_inc(w_hi_done, 1)

        for q in range(NQ):
            for bank in range(2):
                act.wait_ge(ssm_done, 2 * q + bank + 1)
                nc.scalar.copy(y_at(q, bank), y_part(q, bank, 1)).then_inc(y_low, 1)
        piece_hi(0)
        act.wait_ge(ssm_done, 2 * NQ)
        piece_hi(1)

        def zc(e, g):
            n = GROUPS * e + g
            if isinstance(e, int) and e == 0:
                act.wait_ge(z_done, 8 + 2 * g + 2)
            need(act, w2_done, n - 3)
            nc.scalar.copy(zc_hi[:, g, :, :], z_cols(e, g)).then_inc(zc_hi_done, 1)

        def turn2_hi(e, par, g):
            need(act, tr2_done, GROUPS * e + g + 1)
            nc.scalar.copy(h2nT_hi[:, par, :, g * P:(g + 1) * P], tr2_bank(e, g)).then_inc(h2nT_hi_done, 1)

        def activate(e, n):
            kind, j, bank = PLAN[n]
            need(act, up_done, UNITS * e + n + 1)
            if kind == SHARED:
                nc.scalar.activation(act_out[:, n % 4, :], ps[bank][:, :], ACT.Silu,
                                     bias=vec[:, C_SB1 + j:C_SB1 + j + 1]).then_inc(act_done, 1)
            else:
                x = (e + (RES - 1)) & (RES - 1) if kind == OLD else e
                nc.scalar.activation(act_out[:, n % 4, :], ps[bank][:, :], ACT.Gelu,
                                     bias=vec[:, bass.ds(C_B1 + 2 * x + j, 1)]).then_inc(act_done, 1)

        def hidden_hi(e, n):
            kind, j, bank = PLAN[n]
            if kind == SHARED:
                need(act, gated, 4 * e + j + 1)
            else:
                need(act, act_done, UNITS * e + n + 1)
            nc.scalar.mul(hid_hi[:, n % 4, :], act_out[:, n % 4, :], 0.5 if kind == SHARED else 0.25
                          ).then_inc(hid_hi_done, 1)

        def slot(e, par, ahead, before):
            for n in range(UNITS):
                if ahead and 1 <= n <= 4:
                    zc(e + 1, n - 1)
                if n == 6:
                    nc.scalar.activation(warm_out[:, 1:2], zero[:, :], ACT.Gelu)
                activate(e, n)
                if n or before:
                    hidden_hi(*((e, n - 1) if n else (e - 1, UNITS - 1)))
                if ahead and 3 <= n <= 6:
                    turn2_hi(e + 1, 1 - par, n - 3)

        for g in range(GROUPS):
            zc(0, g)
        nc.scalar.activation(warm_out[:, 1:2], zero[:, :], ACT.Gelu)
        piece_hi(2)
        piece_hi(3)
        for g in range(GROUPS):
            turn2_hi(0, 0, g)
            piece_hi(4 + g)
        piece_hi(8)
        slot(0, 0, True, False)
        with act.Fori(0, 3) as i:
            slot(2 * i + 1, 1, True, True)
            slot(2 * i + 2, 0, True, True)
        slot(RES - 1, 1, False, True)
        hidden_hi(RES - 1, UNITS - 1)

    @block.vector
    def _(dve):
        nc.vector.memset(x_pad[:, :, :, :], 0.0).then_inc(pad_zero, 1)
        nc.vector.memset(k_row[:, :, :, :].rearrange("p n c w -> p (n c w)").bitcast(F32), 0.0).then_inc(row_zero, 1)

        steps = 0

        def link(ins):
            nonlocal steps
            steps += 1
            ins.then_inc(k_step, 1)
            dve.wait_ge(k_step, steps)

        dve.wait_ge(vec_in, 16)
        for half in range(HALVES):
            nc.vector.tensor_tensor(mid_bias[:, half:half + 1], vec[:, C_W1B + half:C_W1B + half + 1],
                                    vec[:, C_CONV + 3 * half + 1:C_CONV + 3 * half + 2], ALU.mult)
        link(nc.vector.tensor_tensor(power[:, :, 0], vec[:, C_B:C_B + 32], vec[:, C_C:C_C + 32], ALU.mult))
        dve.wait_ge(abar_done, 1)

        def double(k, first=0, n_states=HALVES * STATES):
            n = 1 << k
            at = slice(first, first + n_states)
            by = abar[:, k, at].rearrange("p (s o) -> p s o", o=1).broadcast_to([P, n_states, n])
            link(nc.vector.tensor_tensor(power[:, at, n:2 * n], power[:, at, 0:n], by, ALU.mult))
            if k < 6:
                link(nc.vector.tensor_tensor(abar[:, k + 1, :], abar[:, k, :], abar[:, k, :], ALU.mult))

        def sum_states(half, t):
            link(nc.vector.tensor_reduce(k_sum[:, half, t:t + HALF],
                                         power[:, half * STATES:(half + 1) * STATES, t:t + HALF]
                                         .rearrange("p s t -> p t s"), AX_X, ALU.add))

        def rows_out():
            link(nc.vector.tensor_tensor(k_sum[:, :, 0], k_sum[:, :, 0], vec[:, C_D:C_D + 2], ALU.add))
            row_hi, row_lo = [k_row[:, SEQ - 1:2 * SEQ - 1, :, w].rearrange("p t c -> p c t") for w in range(2)]
            dve.wait_ge(row_zero, 1)
            link(nc.vector.tensor_copy(row_hi, k_sum[:, :, :]))
            link(nc.vector.tensor_tensor(row_lo, k_sum[:, :, :], row_hi, ALU.subtract))
            assert steps == K_STEPS

        for k in range(5):
            double(k)
        dve.wait_ge(wa_hi, 1)
        nc.vector.tensor_tensor(proj_lo[:, :, :].rearrange("p k n -> p (k n)"), raw_a[:, 0:KC * D],
                                f32(proj_hi[:, :, :].rearrange("p k n -> p (k n)")), ALU.subtract).then_inc(wa_lo, 1)
        beside_cat = {0: lambda: double(5), 1: lambda: double(6, 0, STATES)}
        beside = {0: lambda: double(6, STATES, STATES), 1: lambda: sum_states(0, 0), 2: lambda: sum_states(0, HALF),
                  3: lambda: sum_states(1, 0), 4: lambda: sum_states(1, HALF), 5: rows_out}

        def cat_lo(i, r):
            need(dve, catT_hi_done, RES * i + r + 1)
            nc.vector.tensor_tensor(catT_lo[:, r % 2, :, :].rearrange("p k n -> p (k n)"), CATP[r % 2][:, 0:CAT],
                                    f32(catT_hi[:, r % 2, :, :].rearrange("p k n -> p (k n)")),
                                    ALU.subtract).then_inc(catT_lo_done, 1)
            if isinstance(i, int) and RES * i + r in beside_cat:
                beside_cat[r]()

        def bn_stats(src, m, s_stats):
            nc.vector.bn_stats(stat[:, m, :], src).then_inc(s_stats, 1)

        def bn_aggr(n, m, s_stats, s_aggr):
            need(dve, s_stats, n + 1, pad_zero)
            nc.vector.bn_aggr(mv[:, m, :], stat[:, m, :]).then_inc(s_aggr, 1)

        def add_eps(n, m, s_aggr, s_eps):
            need(dve, s_aggr, n + 1)
            nc.vector.tensor_scalar(rstd[:, m:m + 1], mv[:, m, 1:2], EPS, None, ALU.add).then_inc(s_eps, 1)

        def normalize(n, src, dst, m, s_rstd, s_out):
            need(dve, s_rstd, n + 1)
            nc.vector.tensor_scalar(dst, src, mv[:, m, 0:1], rstd[:, m:m + 1], ALU.subtract, ALU.mult).then_inc(s_out, 1)

        def stats(i, r):
            n = RES * i + r
            need(dve, h_done, n + 1, pad_zero)
            bn_stats(h_ring[:, r % 4, :], r % 4, stats_done)

        def aggr(i, r):
            bn_aggr(RES * i + r, r % 4, stats_done, aggr_done)

        def eps(i, r):
            add_eps(RES * i + r, r % 4, aggr_done, eps_done)

        def norm(i, r):
            n = RES * i + r
            m = r % 4
            if isinstance(i, int) and i == 0:
                dve.wait_ge(rstd_done, n + 1)
                nc.vector.scalar_tensor_tensor(shift[:, m:m + 1], mv[:, m, 0:1], -1.0, rstd[:, m:m + 1], ALU.mult,
                                               ALU.mult).then_inc(shift_done, 1)
            else:
                normalize(n, h_ring[:, m, :], hn[:, m, :], m, rstd_done, hn_done)
            if isinstance(i, int) and n in beside:
                beside[n]()

        def hn_lo(i, pair):
            need(dve, hnT_hi_done, 4 * i + pair + 1)
            nc.vector.tensor_tensor(hnT_at(hnT_lo, i, pair), hn_bank(), f32(hnT_at(hnT_hi, i, pair)),
                                    ALU.subtract).then_inc(hnT_lo_done, 1)

        def x_lo_part(i, u):
            need(dve, x_hi_done, 4 * i + u + 1)
            nc.vector.tensor_tensor(x_at(x_lo, i, u), x_bank(), x_at(x_hi, i, u), ALU.subtract).then_inc(x_lo_done, 1)

        def conv_before(i, g):
            c = C_CONV + 3 * (g % 2)
            need(dve, mm_evac, 8 * i + X1_AT[g] + 1)
            nc.vector.scalar_tensor_tensor(x_mid[:, g % 2, :, :], x_pad[:, g % 2, :, 0:SEQ], vec[:, c:c + 1],
                                           x_mid[:, g % 2, :, :], ALU.mult, ALU.add).then_inc(conv_left, 1)

        def conv_after(i, g):
            c = C_CONV + 3 * (g % 2)
            need(dve, conv_left, 4 * i + g + 1)
            nc.vector.scalar_tensor_tensor(x_mid[:, g % 2, :, :], x_pad[:, g % 2, :, 2:SEQ + 2], vec[:, c + 2:c + 3],
                                           x_mid[:, g % 2, :, :], ALU.mult, ALU.add).then_inc(conv_done, 1)

        run_phase_a(dve, {"cat": cat_lo, "stats": stats, "norm": norm, "aggr": aggr, "conv_left": conv_before, "eps": eps,
                            "conv_right": conv_after, "hn": hn_lo, "x": x_lo_part})

        def piece_lo(n):
            dve.wait_ge(w_hi_done, n + 1)
            nc.vector.tensor_tensor(los[n], raws[n], f32(his[n]), ALU.subtract).then_inc(w_lo_done[0], 1)

        def z_part(u):
            half, k = u // 8, u % 8
            dve.wait_ge(yt_filled, u + 1)
            at = v_sb[:, half, k * BLK:(k + 1) * BLK]
            nc.vector.tensor_tensor(at, yt_bank(u)[:, :], at, ALU.mult).then_inc(z_done, 1)

        for q in range(NQ):
            for bank in range(2):
                dve.wait_ge(y_low, 2 * q + bank + 1)
                nc.vector.tensor_tensor(y_at(q, bank), y_part(q, bank, 0), y_at(q, bank), ALU.add).then_inc(y_done, 1)
            if q > NQ // 2:
                z_part(q - NQ // 2 - 1)
        z_part(NQ // 2 - 1)

        def mixer_out(e, par, g):
            n = GROUPS * e + g
            need(dve, w2_done, n + 1)
            need(dve, h_biased, e + 1)
            if g == 0:
                need(dve, o_done, GROUPS * (e - 1))
            at = h2_sb[:, par, g, :]
            nc.vector.tensor_tensor(at, w2_bank(e, g)[:, 0:D], h_in[:, par, g, :], ALU.add).then_inc(h2_done, 1)
            need(dve, h2_done, n + 1, pad_zero)
            bn_stats(at, g, stats2_done)

        def mixer_stats(e, g):
            n = GROUPS * e + g
            bn_aggr(n, g, stats2_done, aggr2_done)
            add_eps(n, g, aggr2_done, eps2_done)

        def mixer_norm(e, par, g):
            normalize(GROUPS * e + g, h2_sb[:, par, g, :], h2n[:, g, :], g, rstd2_done, h2n_done)

        def turn2_lo(e, par, g):
            need(dve, h2nT_hi_done, GROUPS * e + g + 1)
            nc.vector.tensor_tensor(h2nT_lo[:, par, :, g * P:(g + 1) * P], tr2_bank(e, g),
                                    f32(h2nT_hi[:, par, :, g * P:(g + 1) * P]), ALU.subtract).then_inc(h2nT_lo_done, 1)

        def gate(e, n):
            kind, j, bank = PLAN[n]
            if kind == SHARED:
                need(dve, act_done, UNITS * e + n + 1)
                nc.vector.scalar_tensor_tensor(act_out[:, n % 4, :], ps[bank + 1][:, :], vec[:, C_SB3 + j:C_SB3 + j + 1],
                                               act_out[:, n % 4, :], ALU.add, ALU.mult).then_inc(gated, 1)

        def hidden_lo(e, n):
            kind, j, bank = PLAN[n]
            need(dve, hid_hi_done, UNITS * e + n + 1)
            nc.vector.scalar_tensor_tensor(hid_lo[:, n % 4, :], act_out[:, n % 4, :], 0.5 if kind == SHARED else 0.25,
                                           f32(hid_hi[:, n % 4, :]), ALU.mult, ALU.subtract).then_inc(hid_lo_done, 1)

        def finish(e, par, times):
            last_slot = isinstance(e, int) and e == RES - 1
            if last_slot:
                dve.wait_ge(l2_half_done, 1)
            else:
                need(dve, l2_done, UNITS * e + UNITS)
            need(dve, h2_biased, GROUPS * e + GROUPS)
            need(dve, stored[par], times)
            for g in range(GROUPS):
                if last_slot and g == 2:
                    dve.wait_ge(l2_done, UNITS * RES)
                nc.vector.tensor_tensor(o_sb[:, par, g, :], ps[4 + g // 2][:, (g % 2) * D:(g % 2 + 1) * D],
                                        h2_sb[:, par, g, :], ALU.add).then_inc(o_done, 1)

        def slot(e, par, ahead, before, times=0):
            for n in range(UNITS):
                if n == 2 and before:
                    finish(e - 1, 1 - par, times)
                if ahead and 2 <= n <= 5:
                    mixer_out(e + 1, 1 - par, n - 2)
                    mixer_stats(e + 1, n - 2)
                gate(e, n)
                if n or before:
                    hidden_lo(*((e, n - 1) if n else (e - 1, UNITS - 1)))
                if ahead and 2 <= n <= 5:
                    mixer_norm(e + 1, 1 - par, n - 2)
                if ahead and 3 <= n <= 6:
                    turn2_lo(e + 1, 1 - par, n - 3)

        for u in range(8, 16):
            z_part(u)
            if u == 9:
                piece_lo(0)
        for g in range(GROUPS):
            mixer_out(0, 0, g)
            if g >= 1:
                mixer_norm(0, 0, g - 1)
            mixer_stats(0, g)
            if g >= 2:
                turn2_lo(0, 0, g - 2)
        piece_lo(2)
        mixer_norm(0, 0, 3)
        turn2_lo(0, 0, 2)
        piece_lo(3)
        turn2_lo(0, 0, 3)
        piece_lo(4)
        piece_lo(5)
        piece_lo(6)
        piece_lo(7)
        slot(0, 0, True, False)
        slot(1, 1, True, True)
        slot(2, 0, True, True)
        with dve.Fori(0, 2) as i:
            slot(2 * i + 3, 1, True, True, 16 * i + 16)
            slot(2 * i + 4, 0, True, True, 16 * i + 16)
        slot(RES - 1, 1, False, True, 16 * 3)
        hidden_lo(RES - 1, UNITS - 1)
        finish(RES - 1, 1, 16 * 3)

    @block.tensor
    def _(pe):
        def three(out_, hi, lo, rhs_hi, rhs_lo, start, stop, shared_bank=False):
            kw = {"skip_group_check": True} if shared_bank else {}
            nc.tensor.matmul(out_, hi, rhs_hi, start=start, stop=False, **kw)
            nc.tensor.matmul(out_, hi, rhs_lo, start=False, stop=False, **kw)
            return nc.tensor.matmul(out_, lo, rhs_hi, start=False, stop=stop, **kw)

        def cat_turn(i, r):
            need(pe, gathered[r], 16 * (i + 1))
            need(pe, catT_lo_done, RES * i + r - 1)
            for k in range(KC):
                last = nc.tensor.transpose(CATP[r % 2][:, k * P:(k + 1) * P], cat[:, r, k * P:(k + 1) * P], ident[:, :])
            last.then_inc(cat_tr, 1)

        def embed(i, r):
            n = RES * i + r
            need(pe, catT_lo_done, n + 1)
            need(pe, h_done, n - 1)
            if isinstance(i, int) and n == 0:
                pe.wait_ge(wa_lo, 1)
            for k in range(KC):
                last = three(EMBP[r % 2][:, 0:D], catT_hi[:, r % 2, k, :], catT_lo[:, r % 2, k, :],
                             proj_hi[:, k, :], proj_lo[:, k, :], k == 0, k == KC - 1)
            last.then_inc(emb_done, 1)

        def hn_turn(i, pair):
            need_hn(pe, i, 2 * pair + 1)
            need(pe, hnT_lo_done, 4 * i + pair)
            for r in range(2):
                for half in range(HALVES):
                    at = (r * HALVES + half) * P
                    last = nc.tensor.transpose(HNP[:, at:at + P], hn[:, (2 * pair + r) % 4, half * P:(half + 1) * P],
                                               ident[:, :])
            last.then_inc(hn_turned, 1)

        def x_turn(i, u, last_one=False):
            if isinstance(i, int) and i == GROUPS - 1 and u == 3 and not last_one:
                return
            need(pe, sil_done, 4 * i + u + 1)
            need(pe, x_lo_done, 4 * i + u)
            for b in range(4):
                last = nc.tensor.transpose(XP[:, b * P:(b + 1) * P], x_sil[:, u, b, :], ident[:, :])
            last.then_inc(x_turned, 1)

        def project(i, at):
            which, g = PROJ[at]
            k, half = g // 2, g % 2
            need(pe, hnT_lo_done, 4 * i + 4)
            need(pe, mm_evac, 8 * i + at - 1)
            if isinstance(i, int) and i == 0 and at == 0:
                pe.wait_ge(wv_lo_done, 2)
            for kk in range(HALVES):
                x_parts = [t[:, bass.ds(i & 1, 1), kk, k * BLK:(k + 1) * BLK].rearrange("p o n -> p (o n)")
                           for t in (hnT_hi, hnT_lo)]
                last = three(MM[at % 2][:, :], wv_hi[:, which, kk, half * P:(half + 1) * P],
                             wv_lo[:, which, kk, half * P:(half + 1) * P], *x_parts, kk == 0, kk == HALVES - 1)
            last.then_inc(mm_done, 1)

        pe.wait_ge(ident_step, 2)
        run_phase_a(pe, {"cat": cat_turn, "emb": embed, "hn": hn_turn, "x": x_turn, "mm": project})

        def y_turn(u):
            half, k = u // 8, u % 8
            if k >= 4:
                pe.wait_ge(z_done, u - 3)
            for b in range(4):
                last = nc.tensor.transpose(yt_bank(u)[:, b * P:(b + 1) * P],
                                           y_sb[:, 4 * k + b, half * P:(half + 1) * P], ident[:, :])
            last.then_inc(yt_filled, 1)

        pe.wait_ge(x_lo_done, 15)
        pe.wait_ge(h_done, RES * GROUPS)
        for q in range(NQ):
            loads = q // TRING
            pe.wait_ge(toep_in[q % TRING], 16 * (1 + 2 * loads))
            for j in range(CH):
                c = q * CH + j
                bank, k = j // (CH // 2), j % (CH // 2)
                if k == 0 and q >= 2:
                    pe.wait_ge(y_done, 2 * (q - 2) + bank + 1)
                at = ps[2 * (q % 2) + bank][:, k * 2 * BATCH:(k + 1) * 2 * BATCH]
                t_hi, t_lo = toep(q)[:, j // 2, :, j % 2, 0], toep(q)[:, j // 2, :, j % 2, 1]
                nc.tensor.matmul(at, t_hi, x_sb[:, c, :, :].rearrange("u w b -> u (w b)"), start=True, stop=False,
                                 skip_group_check=True)
                last = nc.tensor.matmul(at[:, 0:BATCH], t_lo, x_hi[:, c, :], start=False, stop=True,
                                        skip_group_check=True)
                if k == CH // 2 - 1:
                    last.then_inc(ssm_done, 1)
            if q == 0:
                x_turn(GROUPS - 1, 3, last_one=True)
            if q == NQ // 2 - 1:
                pe.wait_ge(x_lo_done, 16)
            if q >= NQ // 2:
                if q == NQ // 2:
                    pe.wait_ge(y_done, NQ)
                y_turn(q - NQ // 2)

        def mixer_mm(e, g):
            n = GROUPS * e + g
            need(pe, zc_lo_done, n + 1)
            if isinstance(e, int) and e == 0:
                need(pe, h2_done, g - 2)
            else:
                need(pe, h2_done, n)
            for k in range(HALVES):
                last = three(w2_bank(e, g)[:, 0:D], zc_hi[:, g, k, :], zc_lo[:, g, k, :],
                             w2_hi[:, k, :], w2_lo[:, k, :], k == 0, k == HALVES - 1)
            last.then_inc(w2_done, 1)

        def mixer_turn(e, g):
            n = GROUPS * e + g
            need(pe, h2n_done, n + 1)
            if isinstance(e, int) and e == 0:
                need(pe, h2nT_lo_done, g - 1)
                need(pe, h2_done, 2)
            else:
                need(pe, h2nT_lo_done, n)
            for half in range(HALVES):
                last = nc.tensor.transpose(tr2_bank(e, g)[:, half, :], h2n[:, g, half * P:(half + 1) * P],
                                           ident[:, :])
            last.then_inc(tr2_done, 1)

        def free_banks(e, n):
            acts, gates = {0: (0, None), 1: (None, 0), 2: (0, None), 3: (2, None), 4: (3, 1), 5: (4, 2), 6: (5, None),
                           7: (None, 3)}[n]
            if acts is not None:
                need(pe, act_done, UNITS * e + acts)
            if gates is not None:
                need(pe, gated, 4 * e + gates)

        def hidden(e, par, n):
            kind, j, bank = PLAN[n]
            free_banks(e, n)
            if kind == NEW and j == 0:
                need(pe, ex_done, e)
            for which in range(2 if kind == SHARED else 1):
                for k in range(HALVES):
                    if kind == SHARED:
                        w_hi = sw_hi[:, 2 * which + k, j * P:(j + 1) * P]
                        w_lo = sw_lo[:, 2 * which + k, j * P:(j + 1) * P]
                    else:
                        m = par if kind == NEW else 1 - par
                        at = slice(k * HR + j * P, k * HR + (j + 1) * P)
                        w_hi, w_lo = ex_hi[m][:, 0, at], ex_lo[m][:, 0, at]
                    last = three(ps[bank + which][:, :], w_hi, w_lo, h2nT_hi[:, par, k, :], h2nT_lo[:, par, k, :],
                                 k == 0, k == HALVES - 1)
            last.then_inc(up_done, 1)

        def second(e, par, n):
            kind, j, bank = PLAN[n]
            need(pe, hid_lo_done, UNITS * e + n + 1)
            if n == 0:
                need(pe, o_done, GROUPS * e)
            if n == 2 and isinstance(e, int) and e == 0:
                pe.wait_ge(w_lo_done[0], LO_BY.count(0))
            if kind == SHARED:
                at = slice(j % 2 * D, (j % 2 + 1) * D)
                w_hi, w_lo = sw_hi[:, 4 + j // 2, at], sw_lo[:, 4 + j // 2, at]
            else:
                m = par if kind == NEW else 1 - par
                w_hi, w_lo = ex_hi[m][:, 1, j * D:(j + 1) * D], ex_lo[m][:, 1, j * D:(j + 1) * D]
            for g in range(GROUPS):
                last = three(ps[4 + g // 2][:, (g % 2) * D:(g % 2 + 1) * D], hid_hi[:, n % 4, g * P:(g + 1) * P],
                             hid_lo[:, n % 4, g * P:(g + 1) * P], w_hi, w_lo, n == 0 and g % 2 == 0, n == UNITS - 1,
                             shared_bank=True)
                if isinstance(e, int) and e == RES - 1 and n == UNITS - 1 and g == 1:
                    last.then_inc(l2_half_done, 1)
            last.then_inc(l2_done, 1)

        def slot(e, par, ahead, before):
            need(pe, h2nT_lo_done, GROUPS * e + GROUPS)
            first_use = {0: (1,), 2: (5,), 6: (8,)} if isinstance(e, int) and e == 0 else {}
            for n in range(UNITS):
                for piece in first_use.get(n, ()):
                    need_piece(pe, piece)
                hidden(e, par, n)
                if ahead and 3 <= n <= 6:
                    mixer_turn(e + 1, n - 3)
                if n >= 2:
                    second(e, par, n - 2)
                elif before:
                    second(e - 1, 1 - par, UNITS - 2 + n)
                if ahead and 1 <= n <= 4:
                    mixer_mm(e + 1, n - 1)

        pe.wait_ge(y_done, 2 * NQ)
        for u in range(8, 16):
            y_turn(u)
        pe.wait_ge(w_lo_done[0], 1)
        for g in range(GROUPS):
            mixer_mm(0, g)
        for g in range(GROUPS):
            mixer_turn(0, g)
        slot(0, 0, True, False)
        with pe.Fori(0, 3) as i:
            slot(2 * i + 1, 1, True, True)
            slot(2 * i + 2, 0, True, True)
        slot(RES - 1, 1, False, True)
        second(RES - 1, 1, UNITS - 2)
        second(RES - 1, 1, UNITS - 1)


def kernel(**inputs):
    import numpy as np
    import concourse.bacc as bacc
    from concourse import mybir as mb
    from concourse.bass_utils import run_bass_kernel_spmd as run

    a = {k: np.asarray(v) for k, v in inputs.items()}

    def tiles(w):
        k, n = w.shape
        return np.ascontiguousarray(w.reshape(k // P, P, n).transpose(1, 0, 2).reshape(P, -1))

    def cols(v):
        v = v.reshape(-1, P, v.size // v.shape[0] if v.ndim > 1 else 1)
        return v.transpose(1, 0, 2).reshape(P, -1)

    def pairs(v):
        return v.reshape(P, -1)

    table = np.zeros((VOCAB, CAT), np.float32)
    proj = np.zeros((CAT, D), np.float32)
    row = col = 0
    for t in range(4):
        e, p = a[f"L0_tok_emb{t}"], a[f"L0_tok_proj{t}"]
        table[row:row + e.shape[0], col:col + e.shape[1]] = e
        proj[col:col + e.shape[1]] = p.T
        row, col = row + e.shape[0], col + e.shape[1]
    small = np.concatenate([cols(a["L0_attn_w1_b"]), cols(a["L0_attn_v1_b"]), cols(a["L0_attn_conv_w"].reshape(D, 3)),
                            pairs(a["L0_attn_A"]), pairs(a["L0_attn_B_ssm"]), pairs(a["L0_attn_C_ssm"]),
                            pairs(a["L0_attn_D_ssm"]), cols(a["L0_ffn_sb1"]), cols(a["L0_ffn_sb3"]),
                            cols(a["L0_ffn_b1"].reshape(-1))], axis=1)
    rows = np.concatenate([a["L0_attn_w2_b"], a["L0_ffn_sb2"], a["L0_ffn_b2"].reshape(-1)])
    w_a = np.concatenate([tiles(proj), tiles(a["L0_attn_w1_w"].T), tiles(a["L0_attn_v1_w"].T)], axis=1)
    w_b = np.concatenate([tiles(a["L0_attn_w2_w"].T), tiles(a["L0_ffn_sw1"]), tiles(a["L0_ffn_sw3"]),
                          tiles(a["L0_ffn_sw2"])], axis=1).reshape(P, 7, BLK)
    w_e = np.stack([np.stack([tiles(a["L0_ffn_w1"][e]), tiles(a["L0_ffn_w2"][e])], axis=1) for e in range(RES)])
    arrays = {"ids": a["x"].reshape(-1), "table": table, "small": small, "rows": rows, "w_a": w_a, "w_b": w_b, "w_e": w_e}
    arrays = {k: np.ascontiguousarray(v) for k, v in arrays.items()}

    nc = bacc.Bacc("TRN2", target_bir_lowering=False, num_devices=1)
    args = [nc.dram_tensor(f"{k}_dram", v.shape, mb.dt.from_np(v.dtype), kind="ExternalInput").ap()
            for k, v in arrays.items()]
    scratch = nc.dram_tensor("kernel_rows_dram", (P, 2 * YLEN), F32, kind="Internal").ap()
    h_rows = nc.dram_tensor("h_rows_dram", (RES, P, GROUPS, D), F32, kind="Internal").ap()
    out = nc.dram_tensor("out_dram", (BATCH * SEQ, D), F32, kind="ExternalOutput").ap()
    tower(nc, *args, scratch, h_rows, out)
    r = run(nc, [{f"{k}_dram": v for k, v in arrays.items()}], core_ids=[0])
    return r.results[0]["out_dram"].reshape(BATCH, SEQ, D)
```
